# Optimizing a Trainium2 kernel written in Bass

```python
import numpy as np
import jax
import jax.numpy as jnp

def _softmax(x, axis=-1):
    return jax.nn.softmax(x, axis=axis)

def _gelu(x):
    return jax.nn.gelu(x, approximate=True)

def _silu(x):
    return jax.nn.silu(x)

def _sigmoid(x):
    return jax.nn.sigmoid(x)

def _layernorm(x, axis=-1, eps=1e-05):
    m = jnp.mean(x, axis=axis, keepdims=True)
    v = jnp.var(x, axis=axis, keepdims=True)
    return (x - m) / jnp.sqrt(v + eps)

def _scatter_add(tgt, idx, src, axis=0):
    return tgt.at[idx].add(src)

def _segment_sum(src, seg, n):
    return jax.ops.segment_sum(src, seg, n)
kernel_name = 'mk_adj_resnorm_d4_adj_r2_a34660'

def setup_inputs(seed: int=0):
    np.random.seed(seed)
    _w = jnp.asarray

    def _rec_inputs():
        import jax
        import jax.numpy as jnp
        _gk = jax.random.key(seed)
        x = 0.5 + 0.2887 * jax.random.normal(jax.random.fold_in(_gk, 1), (2048, 256), jnp.float32)
        _a = jax.random.bernoulli(jax.random.fold_in(_gk, 2), 0.0078125, (2048, 2048))
        _a = jnp.logical_or(_a, jnp.eye(2048, dtype=bool))
        _af = _a.astype(jnp.float32)
        _af = _af * jax.random.uniform(jax.random.fold_in(_gk, 3), (2048, 2048), jnp.float32, 0.05, 1)
        adj = _af
        return (x, adj)
    x, adj = _rec_inputs()

    def _L0_gnn_setup():
        import jax, jax.numpy as jnp
        import numpy as np
        N = 4096
        IN_C = 256
        OUT_C = 256
        key = jax.random.key(seed)
        k1, k2, k3 = jax.random.split(key, 3)
        adj_matrix = jax.random.uniform(k1, (N, N), dtype=jnp.float32)
        x = jax.random.uniform(k2, (N, IN_C), dtype=jnp.float32)
        weight = jax.random.uniform(k3, (IN_C, OUT_C), dtype=jnp.float32) / 4 - 0.125
        return {'x': x, 'adj_matrix': adj_matrix, 'weight': weight}
    _L0_gnn_all = _L0_gnn_setup()
    _L0_gnn_in = {k: v for k, v in _L0_gnn_all.items() if k in ('weight',)}
    del _L0_gnn_all

    def _L1_gnn_setup():
        import jax, jax.numpy as jnp
        import numpy as np
        N = 4096
        D = 256
        EPS = 1e-12
        key = jax.random.key(seed)
        k1, k2 = jax.random.split(key)
        cur = jax.random.normal(k1, (N, D), dtype=jnp.float32)
        incidence_m = jax.random.normal(k2, (N, N), dtype=jnp.float32)
        return {'cur': cur, 'incidence_m': incidence_m}
    _L1_gnn_all = _L1_gnn_setup()
    _L1_gnn_in = {k: v for k, v in _L1_gnn_all.items() if k in ()}
    del _L1_gnn_all

    def _L2_gnn_setup():
        import jax, jax.numpy as jnp
        import numpy as np
        N = 4096
        D = 256
        key = jax.random.key(seed)
        ks = jax.random.split(key, 6)
        s = 1.0 / np.sqrt(D)
        return {'x': jax.random.normal(ks[0], (N, D), jnp.float32), 'spatial_encoding': jax.random.normal(ks[1], (N, N), jnp.float32), 'edge_encoding': jax.random.normal(ks[2], (N, N), jnp.float32), 'Wq': jax.random.normal(ks[3], (D, D), jnp.float32) * s, 'bq': jnp.zeros((D,), jnp.float32), 'Wk': jax.random.normal(ks[4], (D, D), jnp.float32) * s, 'bk': jnp.zeros((D,), jnp.float32), 'Wv': jax.random.normal(ks[5], (D, D), jnp.float32) * s, 'bv': jnp.zeros((D,), jnp.float32)}
    _L2_gnn_all = _L2_gnn_setup()
    _L2_gnn_in = {k: v for k, v in _L2_gnn_all.items() if k in ('Wq', 'bq', 'Wk', 'bk', 'Wv', 'bv')}
    del _L2_gnn_all

    def _L3_gnn_setup():
        import jax, jax.numpy as jnp
        import numpy as np
        N = 2048
        INPUT_DIM = 256
        KEY_DIM = 64
        OUT_DIM = 256
        N_HEADS = 8
        IDENTITY_BIAS = 0.01
        MASK_VAL = 1e+16

        def _xavier(key, shape, gain=np.sqrt(2.0)):
            std = gain * np.sqrt(2.0 / (shape[-2] + shape[-1]))
            return jax.random.normal(key, shape, dtype=jnp.float32) * np.float32(std)
        key = jax.random.key(seed)
        kx, ka, kk, kq, kv, ko = jax.random.split(key, 6)
        node_matrix = jax.random.normal(kx, (N, INPUT_DIM), dtype=jnp.float32)
        adjacency_matrix = jax.random.bernoulli(ka, 0.01, (N, N)).astype(jnp.float32)
        Wks = _xavier(kk, (N_HEADS, INPUT_DIM, KEY_DIM))
        Wqs = _xavier(kq, (N_HEADS, INPUT_DIM, KEY_DIM))
        Wvs = _xavier(kv, (N_HEADS, INPUT_DIM, KEY_DIM))
        Wo = _xavier(ko, (N_HEADS, KEY_DIM, OUT_DIM))
        return {'node_matrix': node_matrix, 'adjacency_matrix': adjacency_matrix, 'Wks': Wks, 'Wqs': Wqs, 'Wvs': Wvs, 'Wo': Wo}
    _L3_gnn_all = _L3_gnn_setup()
    _L3_gnn_in = {k: v for k, v in _L3_gnn_all.items() if k in ('Wks', 'Wqs', 'Wvs', 'Wo')}
    del _L3_gnn_all
    return {'x': x, 'adj': adj, 'L0_gnn_weight': _L0_gnn_in['weight'], 'L2_gnn_Wq': _L2_gnn_in['Wq'], 'L2_gnn_bq': _L2_gnn_in['bq'], 'L2_gnn_Wk': _L2_gnn_in['Wk'], 'L2_gnn_bk': _L2_gnn_in['bk'], 'L2_gnn_Wv': _L2_gnn_in['Wv'], 'L2_gnn_bv': _L2_gnn_in['bv'], 'L3_gnn_Wks': _L3_gnn_in['Wks'], 'L3_gnn_Wqs': _L3_gnn_in['Wqs'], 'L3_gnn_Wvs': _L3_gnn_in['Wvs'], 'L3_gnn_Wo': _L3_gnn_in['Wo']}

def reference(x, adj, L0_gnn_weight, L2_gnn_Wq, L2_gnn_bq, L2_gnn_Wk, L2_gnn_bk, L2_gnn_Wv, L2_gnn_bv, L3_gnn_Wks, L3_gnn_Wqs, L3_gnn_Wvs, L3_gnn_Wo):
    import jax
    import jax.numpy as jnp

    def _L0_gnn_ref(x, adj_matrix, weight):
        import jax, jax.numpy as jnp
        import numpy as np
        N = 4096
        IN_C = 256
        OUT_C = 256
        n = adj_matrix.shape[0]
        deg = jnp.sum(adj_matrix, axis=1)
        dinv = (deg + 1.0) ** (-0.5)
        aug = dinv[:, None] * (adj_matrix + jnp.eye(n, dtype=adj_matrix.dtype)) * dinv[None, :]
        return jax.nn.relu(aug @ x @ weight)

    def _L1_gnn_ref(cur, incidence_m):
        import jax, jax.numpy as jnp
        import numpy as np
        N = 4096
        D = 256
        EPS = 1e-12
        mask = incidence_m > 0
        head = jax.lax.stop_gradient(mask.astype(incidence_m.dtype))
        head = head / jnp.maximum(jnp.sqrt(jnp.sum(head * head, axis=-1, keepdims=True)), EPS)
        inc = incidence_m + head
        edge_fea = inc @ cur
        edge_degree = jnp.sum(inc, axis=-1, keepdims=True)
        return edge_fea / edge_degree

    def _L2_gnn_ref(x, spatial_encoding, edge_encoding, Wq, bq, Wk, bk, Wv, bv):
        import jax, jax.numpy as jnp
        import numpy as np
        N = 4096
        D = 256
        q = x @ Wq.T + bq
        k = x @ Wk.T + bk
        v = x @ Wv.T + bv
        scale = 1.0 / jnp.sqrt(jnp.asarray(q.shape[-1], q.dtype))
        a = q @ k.T * scale + spatial_encoding + edge_encoding
        attn = jax.nn.softmax(a, axis=-1)
        return attn @ v

    def _L3_gnn_ref(node_matrix, adjacency_matrix, Wks, Wqs, Wvs, Wo):
        import jax, jax.numpy as jnp
        import numpy as np
        N = 2048
        INPUT_DIM = 256
        KEY_DIM = 64
        OUT_DIM = 256
        N_HEADS = 8
        IDENTITY_BIAS = 0.01
        MASK_VAL = 1e+16

        def _xavier(key, shape, gain=np.sqrt(2.0)):
            std = gain * np.sqrt(2.0 / (shape[-2] + shape[-1]))
            return jax.random.normal(key, shape, dtype=jnp.float32) * np.float32(std)
        n = node_matrix.shape[0]
        kd = Wks.shape[-1]
        eye = jnp.eye(n, dtype=node_matrix.dtype)
        adj = jnp.maximum(adjacency_matrix, eye)
        q = jnp.einsum('nd,hdk->hnk', node_matrix, Wqs)
        k = jnp.einsum('nd,hdk->hnk', node_matrix, Wks)
        v = jnp.einsum('nd,hdk->hnk', node_matrix, Wvs)
        scores = jnp.einsum('hqk,hmk->hqm', q, k) * kd ** (-0.5)
        scores = scores + IDENTITY_BIAS * eye - MASK_VAL * (1.0 - adj)
        att = jax.nn.softmax(scores, axis=-1)
        return jnp.einsum('hqm,hmk,hko->qo', att, v, Wo)
    x = _layernorm(x + _L0_gnn_ref(x, adj, L0_gnn_weight), axis=-1)
    x = _layernorm(x + _L1_gnn_ref(x, adj), axis=-1)
    x = _layernorm(x + _L2_gnn_ref(x, adj, adj, L2_gnn_Wq, L2_gnn_bq, L2_gnn_Wk, L2_gnn_bk, L2_gnn_Wv, L2_gnn_bv), axis=-1)
    x = _layernorm(x + _L3_gnn_ref(x, adj, L3_gnn_Wks, L3_gnn_Wqs, L3_gnn_Wvs, L3_gnn_Wo), axis=-1)
    return x

_drawn_inputs = setup_inputs


def setup_inputs(seed=0):
    import zlib

    import numpy as np

    out = dict(_drawn_inputs(seed))
    spreads = {'L2_gnn_bq': (0.0, 0.8), 'L2_gnn_bk': (0.0, 0.8), 'L2_gnn_bv': (0.0, 0.1)}
    factors = {'L2_gnn_Wq': 3.755, 'L2_gnn_Wk': 3.693}
    for name, (base, spread) in spreads.items():
        noise = np.random.default_rng([zlib.crc32(name.encode()), seed]).standard_normal(out[name].shape)
        drawn = base * np.exp(spread * noise) if base else spread * noise
        out[name] = jnp.asarray(drawn.astype(out[name].dtype))
    for name, factor in factors.items():
        out[name] = (out[name] * factor).astype(out[name].dtype)
    return out
```

```python
import concourse.bass as bass
from concourse import mybir
from contextlib import ExitStack

F32 = mybir.dt.float32
F32R = mybir.dt.float32r
I32 = mybir.dt.int32
ALU = mybir.AluOpType
ACT = mybir.ActivationFunctionType
AX = mybir.AxisListType

P = 128
N = 2048
D = 256
TILES = N // P
DC = D // P
BLK = 512
CHUNKS = N // BLK
SUB = BLK // P
HEADS = 8
KD = 64
HK = HEADS * KD
LN_EPS = 1e-5
EDGE_EPS = 1e-12
ATT_SCALE = float(D) ** -0.5
HEAD_SCALE = float(KD) ** -0.5
IDENTITY_BIAS = 0.01
MASK_VAL = 1e16
LOWEST = -3.0e38
NORMS_BOUND = (1e8 / (D * HEAD_SCALE)) ** 2


def active(t, lag, count=TILES):
    return not isinstance(t, int) or lag <= t < count + lag


def wait(eng, sem, value):
    if not isinstance(value, int) or value > 0:
        eng.wait_ge(sem, value)


def own_instruction(eng, held):
    eng.sem_inc(held, 1)


def over_tiles(eng, step, lag=0, count=TILES, peel=2):
    for t in range(peel):
        step(t, t % 2)
    with eng.Fori(peel // 2, count // 2) as pair:
        step(pair * 2, 0)
        step(pair * 2 + 1, 1)
    for t in range(count, count + lag):
        step(t, t % 2)


def loaded(t, s):
    return (t - s) * 8 + 16


def tile_cols(t):
    return bass.ds(t * P, P)


def f32(ap):
    return ap.bitcast(F32)


def build(nc, x, xT, adj, adjT, adj_diag, w0, wqT, bq, wkT, bk, wvT, bv, hwk, hwq, hwv, hwvT, hwo, hwo_rows, ident_in, out):
    with ExitStack() as ctx:
        def sb(name, shape, dt=F32):
            return ctx.enter_context(nc.sbuf_tensor(name, shape, dt))

        def sem(name):
            return ctx.enter_context(nc.semaphore(name))

        X = sb("X", [P, TILES, D])
        XT = sb("XT", [P, DC, N])
        opA_hi = sb("opA_hi", [P, TILES, D], F32R)
        opA_lo = sb("opA_lo", [P, TILES, D], F32R)
        opB_hi = sb("opB_hi", [P, TILES, D], F32R)
        opB_lo = sb("opB_lo", [P, TILES, D], F32R)
        keyT_hi = sb("keyT_hi", [P, DC, N], F32R)
        keyT_lo = sb("keyT_lo", [P, DC, N], F32R)
        raw = sb("raw", [P, 2, N])
        part_hi = sb("part_hi", [P, CHUNKS, BLK], F32R)
        part_lo = sb("part_lo", [P, CHUNKS, BLK], F32R)
        edges = sb("edges", [P, CHUNKS, BLK], F32R)
        w0_sb = sb("w0_sb", [P, DC, D])
        wqT_sb = sb("wqT_sb", [P, DC, D])
        wkT_sb = sb("wkT_sb", [P, DC, D])
        wvT_sb = sb("wvT_sb", [P, DC, D])
        bq_sb = sb("bq_sb", [P, DC])
        bk_sb = sb("bk_sb", [P, DC])
        bv_sb = sb("bv_sb", [P, D])
        stage = sb("stage", [P, 2, HK * D // P])
        wvo_sb = sb("wvo_sb", [P, DC, D])
        ident = sb("ident", [P, P])
        ident_r = sb("ident_r", [P, P], F32R)
        ones = sb("ones", [P, P])
        deg = sb("deg", [P, TILES])
        count = sb("count", [P, TILES])
        full = sb("full", [P, TILES])
        diag = sb("diag", [P, TILES])
        diag_full = sb("diag_full", [P, TILES])
        deg1 = sb("deg1", [P, TILES])
        count_safe = sb("count_safe", [P, TILES])
        head_sum = sb("head_sum", [P, TILES])
        edge_deg = sb("edge_deg", [P, TILES])
        dinv = sb("dinv", [P, TILES])
        rcount = sb("rcount", [P, TILES])
        redge = sb("redge", [P, TILES])
        minus_half = sb("minus_half", [P, TILES])
        ln_eps = sb("ln_eps", [P, 1])
        sums = sb("sums", [P, 4])
        full_rows = sb("full_rows", [P, 2])
        flag = sb("flag", [1, 8])
        flag_int = sb("flag_int", [1, 1], I32)
        branch = sb("branch", [P, D])
        ysum = sb("ysum", [P, 2, D])
        xn = sb("xn", [P, 2, D])
        stats = sb("stats", [P, 2, 6])
        mv = sb("mv", [P, 2, 2])
        veps = sb("veps", [P, 2, 1])
        rstd = sb("rstd", [P, 2, 1])
        xT_tile = sb("xT_tile", [P, 2, DC, P])
        vf = sb("vf", [P, D])
        qf = sb("qf", [P, DC, P])
        q_hi = sb("q_hi", [P, DC, P], F32R)
        q_lo = sb("q_lo", [P, DC, P], F32R)
        mx = sb("mx", [P, CHUNKS])
        nmax = sb("nmax", [P, 2, 1])
        wsum = sb("wsum", [P, 2, 1])
        rsum = sb("rsum", [P, 1])
        y3 = sb("y3", [P, D])
        stats3 = sb("stats3", [P, 6])
        mv3 = sb("mv3", [P, 2])
        veps3 = sb("veps3", [P, 1])
        rstd3 = sb("rstd3", [P, 1])
        out_tile = sb("out_tile", [P, 2, D])

        wide = ctx.enter_context(nc.psum_tensor("wide", [P, CHUNKS, BLK], F32))
        bank = [ctx.enter_context(nc.psum_tensor(f"bank{i}", [P, BLK], F32)) for i in range(4)]

        def xw_out(t):
            half = slice((t % 2) * D, (t % 2 + 1) * D)
            return wide[:, t // 2, half] if t < 8 else bank[t // 2 - 4][:, half]

        wvo_out = [bank[3][:, c * D:(c + 1) * D] for c in range(DC)]
        totals = bank[2][0:1, 0:4]
        acc_weighted = [wide[:, s, 0:D] for s in range(2)]
        acc_edges = [wide[:, 2 + s, 0:D] for s in range(2)]
        xT_out1 = bank[0][:, 0:D].rearrange("p (c q) -> p c q", c=DC)
        key_out = bank[1][:, 0:D].rearrange("p (c q) -> p c q", c=DC)
        value_out = bank[2][:, 0:D]
        q_out = bank[3][:, 0:D].rearrange("p (c q) -> p c q", c=DC)
        xT_out2 = bank[3][:, D:2 * D].rearrange("p (c q) -> p c q", c=DC)
        attended = bank[2][:, 0:D]
        mixed = bank[2][:, D:2 * D]

        xT_in, w_in, stage_vo_in, stage_qk_in = (sem(n) for n in ("xT_in", "w_in", "stage_vo_in", "stage_qk_in"))
        row_in = [sem(f"row_in{s}") for s in range(2)]
        row_summed, row_counted, row_full = sem("row_summed"), sem("row_counted"), sem("row_full")
        dve_held, pe_held = sem("dve_held"), sem("pe_held")
        consts, ident_ready = sem("consts"), sem("ident_ready")
        xw_done, wvo_ps, wvo_ready = sem("xw_done"), sem("wvo_ps"), sem("wvo_ready")
        norms_done, degree_step, flag_step = sem("norms_done"), sem("degree_step"), sem("flag_step")
        pow_done, z_hi, z_lo, totals_done = sem("pow_done"), sem("z_hi"), sem("z_lo"), sem("totals_done")

        def named(prefix, names):
            return {n: sem(f"{prefix}_{n}") for n in names.split()}

        L0 = named("l0", "in0 in1 hi lo chunk_used acc branch y stats mv veps rstd xn rows op_hi op_lo")
        L1 = named("l1", "in0 in1 hi lo edges chunk_used branch sum y stats mv veps rstd xn rows "
                         "xT_ps xT xT_all key_ps key_hi key_lo value_ps value value_hi value_lo")
        L2 = named("l2", "in0 in1 q_ps qf q_hi q_lo scores masked mx nmax exp tr_ps w_hi w_lo attended "
                         "rsum y stats mv veps rstd xn rows xT_ps xT xT_all mixed "
                         "y3 stats3 mv3 veps3 rstd3 out stored0 stored1")

        G = named("l3", "weights key_ps key_hi key_lo value_ps value_hi value_lo adj_in q_ps qf q_hi q_lo "
                        "scores penalty taken masked mx exp tr_ps w_hi w_lo attended rsum head head_t_ps head_t mixed "
                        "added stats mv veps rstd normed stored0 stored1 zeroed")

        head_wq, head_wk, head_wv = (stage[:, 0, k * DC * KD:(k + 1) * DC * KD].rearrange("p (c k) -> p c k", c=DC)
                                     for k in range(3))
        head_wo = stage[0:KD, 1, 0:D]
        head_key_hi, head_key_lo = keyT_hi[0:KD, 0, :], keyT_lo[0:KD, 0, :]
        head_value_hi, head_value_lo = opA_hi[:, :, 0:KD], opA_lo[:, :, 0:KD]
        head_qf, head_q_hi, head_q_lo = qf[0:KD, 0, :], q_hi[0:KD, 0, :], q_lo[0:KD, 0, :]
        head_key_out = wide[0:KD, :, :]
        head_value_out = [bank[2 + k][:, :].rearrange("p (t k) -> p t k", t=TILES // 2) for k in range(2)]
        head_q_out = bank[3][0:KD, 0:P]
        head_attended = bank[2][:, 0:KD]
        head_padded = vf[:, 0:P]
        head_T_out, head_T = bank[3][:, 0:P], qf[:, 1, :]
        head_mixed = bank[2][:, 0:D]
        scores_sb, adj_sb = raw[:, 0, :], raw[:, 1, :]

        def needed(eng):
            eng.wait_ge(flag_step, 7)
            return eng.value_load(flag_int[0:1, 0:1], min_val=0, max_val=N * N + 1) >= 1

        def heads_and_tiles(eng, per_head, per_tile):
            with eng.Fori(0, HEADS) as h:
                per_head(h)
                with eng.Fori(0, TILES) as t:
                    per_tile(h * TILES + t, t)

        block = ctx.enter_context(nc.Block())

        @block.sync
        def _(sp):
            def rows(t, s):
                wait(sp, row_summed, t - 1)
                wait(sp, row_full, t - 1)
                sp.dma_start(raw[:, s, :], adj[tile_cols(t), :]).then_inc(row_in[s], 16)

            over_tiles(sp, rows)

            def blocks0(t, s):
                if isinstance(t, int) and t < 2:
                    sp.wait_ge(row_summed, TILES - 1 + t)
                    sp.wait_ge(row_full, TILES - 1 + t)
                wait(sp, L0["lo"], (t - 1) * CHUNKS)
                sp.dma_start(raw[:, s, :], adjT[tile_cols(t), :]).then_inc(L0[f"in{s}"], 16)

            over_tiles(sp, blocks0)

            def blocks1(t, s):
                if isinstance(t, int) and t < 2:
                    sp.wait_ge(L0["lo"], (TILES - 1 + t) * CHUNKS)
                wait(sp, L1["lo"], (t - 1) * CHUNKS)
                wait(sp, L1["edges"], (t - 1) * CHUNKS)
                sp.dma_start(raw[:, s, :], adjT[tile_cols(t), :]).then_inc(L1[f"in{s}"], 16)

            over_tiles(sp, blocks1)

            def attention(t, s):
                if active(t, 4):
                    u = t - 4
                    sp.wait_ge(L2["out"], u + 1)
                    sp.dma_start(out[tile_cols(u), :], out_tile[:, s, :]).then_inc(L2[f"stored{s}"], 16)
                if active(t, 0):
                    if isinstance(t, int) and t < 2:
                        sp.wait_ge(L1["lo"], (TILES - 1 + t) * CHUNKS)
                        sp.wait_ge(L1["edges"], (TILES - 1 + t) * CHUNKS)
                    wait(sp, L2["tr_ps"], (t - 1) * CHUNKS)
                    sp.dma_start(raw[:, s, :], adj[tile_cols(t), :]).then_inc(L2[f"in{s}"], 16)

            over_tiles(sp, attention, lag=4, peel=4)
            for s in range(2):
                sp.wait_ge(L2[f"stored{s}"], 16 * TILES // 2)

            with sp.If(needed(sp)):
                def weights(h):
                    sp.wait_ge(G["added"], h * TILES + 1)
                    for dst, src in ((head_wq, hwq), (head_wk, hwk), (head_wv, hwv)):
                        sp.dma_start(dst, src.rearrange("p (c h k) -> p c h k", c=DC, h=HEADS)[:, :, h, :])\
                            .then_inc(G["weights"], 16)
                    sp.dma_start(head_wo, hwo_rows[bass.ds(h * KD, KD), :]).then_inc(G["weights"], 16)

                def adjacency(n, t):
                    sp.wait_ge(G["taken"], n + 1)
                    sp.dma_start(adj_sb, adj[tile_cols(t), :]).then_inc(G["adj_in"], 16)

                heads_and_tiles(sp, weights, adjacency)
                with sp.Fori(0, TILES // 2) as pair:
                    for s in range(2):
                        sp.wait_ge(G["normed"], pair * 2 + s + 1)
                        sp.dma_start(out[tile_cols(pair * 2 + s), :], out_tile[:, s, :])\
                            .then_inc(G[f"stored{s}"], 16)
                for s in range(2):
                    sp.wait_ge(G[f"stored{s}"], 16 * TILES // 2 + 16)

        @block.gpsimd
        def _(pool):
            nc.gpsimd.memset(minus_half[:, :], -0.5).then_inc(consts, 1)
            nc.gpsimd.memset(ones[:, :], 1.0).then_inc(consts, 1)
            nc.gpsimd.memset(sums[:, :], 0.0).then_inc(consts, 1)
            nc.gpsimd.memset(ln_eps[:, :], LN_EPS).then_inc(consts, 1)
            pool.wait_ge(consts, 4)
            pool.wait_ge(degree_step, 2)
            nc.gpsimd.tensor_tensor(dinv[:, :], deg1[:, :], minus_half[:, :], ALU.pow).then_inc(pow_done, 1)
            nc.gpsimd.tensor_tensor(rcount[:, :], count_safe[:, :], minus_half[:, :], ALU.pow).then_inc(pow_done, 1)

            def norm_scale(L, t, s):
                pool.wait_ge(L["mv"], t + 1)
                nc.gpsimd.tensor_tensor(veps[:, s, :], mv[:, s, 1:2], ln_eps[:, :], ALU.add).then_inc(L["veps"], 1)
                pool.wait_ge(L["veps"], t + 1)
                nc.gpsimd.tensor_tensor(rstd[:, s, :], veps[:, s, :], minus_half[:, 0:1], ALU.pow)\
                    .then_inc(L["rstd"], 1)

            def keep_rows(L, t, s):
                pool.wait_ge(L["xn"], t + 1)
                nc.gpsimd.tensor_copy(X[:, t, :], xn[:, s, :]).then_inc(L["rows"], 1)

            def step0(t, s):
                norm_scale(L0, t, s)
                keep_rows(L0, t, s)

            over_tiles(pool, step0)

            def step1(t, s):
                norm_scale(L1, t, s)
                keep_rows(L1, t, s)
                pool.wait_ge(L1["xT"], t + 1)
                nc.gpsimd.tensor_copy(XT[:, :, tile_cols(t)], xT_tile[:, s, :, :]).then_inc(L1["xT_all"], 1)

            over_tiles(pool, step1)

            def step2(t, s):
                if active(t, 1):
                    u = t - 1
                    pool.wait_ge(L2["mv3"], u + 1)
                    nc.gpsimd.tensor_tensor(veps3[:, :], mv3[:, 1:2], ln_eps[:, :], ALU.add)\
                        .then_inc(L2["veps3"], 1)
                    pool.wait_ge(L2["veps3"], u + 1)
                    nc.gpsimd.tensor_tensor(rstd3[:, :], veps3[:, :], minus_half[:, 0:1], ALU.pow)\
                        .then_inc(L2["rstd3"], 1)
                if active(t, 0):
                    norm_scale(L2, t, s)
                    keep_rows(L2, t, s)

                if active(t, 1):
                    u = t - 1
                    pool.wait_ge(L2["xT"], u + 1)
                    nc.gpsimd.tensor_copy(XT[:, :, tile_cols(u)], xT_tile[:, 1 - s, :, :]).then_inc(L2["xT_all"], 1)

            over_tiles(pool, step2, lag=1)

            with pool.If(needed(pool)):
                with pool.Fori(0, TILES) as t:
                    pool.wait_ge(G["mv"], t + 1)
                    nc.gpsimd.tensor_tensor(veps3[:, :], mv3[:, 1:2], ln_eps[:, :], ALU.add).then_inc(G["veps"], 1)
                    pool.wait_ge(G["veps"], t + 1)
                    nc.gpsimd.tensor_tensor(rstd3[:, :], veps3[:, :], minus_half[:, 0:1], ALU.pow)\
                        .then_inc(G["rstd"], 1)

        @block.scalar
        def _(act):
            for dst, src in ((XT[:, :, :], xT), (w0_sb[:, :, :], w0)):
                act.dma_start(dst, src).then_inc(xT_in, 16)
            for s, src in ((0, hwvT), (1, hwo)):
                act.dma_start(stage[:, s, :], src).then_inc(stage_vo_in, 16)
            weights = ((X[:, :, :], x), (wqT_sb[:, :, :], wqT), (wkT_sb[:, :, :], wkT), (wvT_sb[:, :, :], wvT),
                       (bq_sb[:, :], bq), (bk_sb[:, :], bk), (bv_sb[:, :], bv), (ident[:, :], ident_in),
                       (diag[:, :], adj_diag))
            for dst, src in weights:
                act.dma_start(dst, src).then_inc(w_in, 16)

            def row_sum(t, s):
                act.wait_ge(row_in[s], loaded(t, s))
                wait(act, row_summed, t)
                nc.scalar.activation(opB_hi[:, 0:8, :].rearrange("p a b -> p (a b)"), raw[:, s, :], ACT.Copy,
                                     accum_out=deg[:, bass.ds(t, 1)]).then_inc(row_summed, 1)

            over_tiles(act, row_sum)
            act.wait_ge(row_summed, TILES)
            act.wait_ge(w_in, 16 * len(weights))
            nc.scalar.activation(ident_r[:, :], ident[:, :], ACT.Copy).then_inc(ident_ready, 1)
            for c in range(DC):
                act.wait_ge(wvo_ps, 1)
                nc.scalar.activation(wvo_sb[:, c, :], wvo_out[c], ACT.Copy).then_inc(wvo_ready, 1)
            for s, src in ((0, hwq), (1, hwk)):
                act.dma_start(stage[:, s, :], src).then_inc(stage_qk_in, 16)
            act.wait_ge(consts, 4)
            for s in range(2):
                act.wait_ge(stage_qk_in, 32)
                wait(act, norms_done, s)
                nc.scalar.activation(opB_hi[:, 0:4, :].rearrange("p a b -> p (a b)"), stage[:, s, :], ACT.Square,
                                     accum_out=sums[:, 1 + s:2 + s]).then_inc(norms_done, 1)
            act.wait_ge(norms_done, 2)
            act.wait_ge(pow_done, 1)
            for t in range(TILES):
                act.wait_ge(xw_done, t // 2 * 2 + 2)
                nc.scalar.activation(opA_hi[:, t, :], xw_out(t), ACT.Copy, scale=dinv[:, t:t + 1])\
                    .then_inc(z_hi, 1)

            def split_hi(L, t, s, q):
                if q == 0:
                    act.wait_ge(L[f"in{s}"], loaded(t, s))
                wait(act, L["chunk_used"], (t - 1) * CHUNKS + q + 1)
                nc.scalar.activation(part_hi[:, q, :], raw[:, s, q * BLK:(q + 1) * BLK], ACT.Copy)\
                    .then_inc(L["hi"], 1)

            def step0(t, s):
                if active(t, 0):
                    for q in range(CHUNKS):
                        split_hi(L0, t, s, q)
                if active(t, 1):
                    u = t - 1
                    act.wait_ge(L0["xn"], u + 1)
                    nc.scalar.activation(opB_hi[:, u, :], xn[:, 1 - s, :], ACT.Copy).then_inc(L0["op_hi"], 1)

            over_tiles(act, step0, lag=1)

            def step1(t, s):
                for q in range(CHUNKS):
                    if active(t, 0):
                        split_hi(L1, t, s, q)
                    if q == 1 and active(t, 1):
                        u = t - 1
                        act.wait_ge(L1["chunk_used"], (u + 1) * CHUNKS)
                        wait(act, L1["sum"], u)
                        nc.scalar.activation(branch[:, :], acc_edges[1 - s], ACT.Copy,
                                             scale=rcount[:, bass.ds(u, 1)]).then_inc(L1["branch"], 1)
                    if q == 1 and active(t, 2):
                        u = t - 2
                        act.wait_ge(L1["key_ps"], u + 1)
                        for c in range(DC):
                            nc.scalar.activation(keyT_hi[:, c, tile_cols(u)], key_out[:, c, :], ACT.Identity,
                                                 bias=bk_sb[:, c:c + 1]).then_inc(L1["key_hi"], 1)
                        act.wait_ge(L1["value"], u + 1)
                        nc.scalar.activation(opA_hi[:, u, :], vf[:, :], ACT.Copy).then_inc(L1["value_hi"], 1)
                if active(t, 1):
                    u = t - 1
                    act.wait_ge(L1["xT_ps"], u + 1)
                    wait(act, L1["value_ps"], u - 1)
                    wait(act, L1["xT_all"], u - 1)
                    nc.scalar.activation(xT_tile[:, 1 - s, :, :], xT_out1, ACT.Copy).then_inc(L1["xT"], 1)

            over_tiles(act, step1, lag=2)

            def step2(t, s):
                if active(t, 0):
                    act.wait_ge(L2["qf"], DC * (t + 1))
                    wait(act, L2["scores"], t)
                    nc.scalar.activation(q_hi[:, :, :], qf[:, :, :], ACT.Copy).then_inc(L2["q_hi"], 1)
                for q in range(CHUNKS):
                    if active(t, 2):
                        u = t - 2
                        act.wait_ge(L2["tr_ps"], u * CHUNKS + q + 1)
                        wait(act, L2["attended"], (u - 1) * CHUNKS + q + 1)
                        nc.scalar.activation(part_hi[:, q, :], bank[q % 2][:, :], ACT.Copy).then_inc(L2["w_hi"], 1)
                    if q == 0 and active(t, 3):
                        u = t - 3
                        act.wait_ge(L2["xT_ps"], u + 1)
                        wait(act, L2["mixed"], u - 1)
                        wait(act, L2["xT_all"], u - 1)
                        act.wait_ge(L2["qf"], DC * (t + 1) if active(t, 0) else DC * TILES)
                        nc.scalar.activation(xT_tile[:, 1 - s, :, :], xT_out2, ACT.Copy).then_inc(L2["xT"], 1)
                    if q == 1 and active(t, 1):
                        u = t - 1
                        act.wait_ge(L2["nmax"], u + 1)
                        wait(act, L2["rsum"], u - 1)
                        nc.scalar.activation(raw[:, 1 - s, :], raw[:, 1 - s, :], ACT.Exp, bias=nmax[:, 1 - s, :],
                                             accum_out=wsum[:, 1 - s, :]).then_inc(L2["exp"], 1)

            over_tiles(act, step2, lag=3, peel=4)

            with act.If(needed(act)):
                def head_operands(h):
                    act.wait_ge(G["key_ps"], h + 1)
                    nc.scalar.activation(head_key_hi, head_key_out, ACT.Copy).then_inc(G["key_hi"], 1)
                    act.wait_ge(G["value_ps"], h + 1)
                    for k in range(2):
                        nc.scalar.activation(head_value_hi[:, k * TILES // 2:(k + 1) * TILES // 2, :],
                                             head_value_out[k], ACT.Copy).then_inc(G["value_hi"], 1)

                def tile(n, t):
                    act.wait_ge(G["qf"], n + 1)
                    nc.scalar.activation(head_q_hi, head_qf, ACT.Copy).then_inc(G["q_hi"], 1)
                    act.wait_ge(G["mx"], 2 * n + 2)
                    nc.scalar.activation(scores_sb, scores_sb, ACT.Exp, bias=nmax[:, 0, :],
                                         accum_out=wsum[:, 0, :]).then_inc(G["exp"], 1)
                    for q in range(CHUNKS):
                        act.wait_ge(G["tr_ps"], n * CHUNKS + q + 1)
                        nc.scalar.activation(part_hi[:, q, :], bank[q % 2][:, :], ACT.Copy).then_inc(G["w_hi"], 1)
                    act.wait_ge(G["head_t_ps"], n + 1)
                    nc.scalar.activation(head_T, head_T_out, ACT.Copy).then_inc(G["head_t"], 1)

                heads_and_tiles(act, head_operands, tile)

        @block.vector
        def _(dve):
            def row_count(t, s):
                dve.wait_ge(row_in[s], loaded(t, s))
                wait(dve, row_full, t)
                nc.vector.tensor_scalar(opB_lo[:, 0:8, :].rearrange("p a b -> p (a b)"), raw[:, s, :], 0.0, 0.0,
                                        ALU.is_gt, ALU.add, accum_out=count[:, bass.ds(t, 1)])\
                    .then_inc(row_counted, 1)
                dve.wait_ge(row_counted, t + 1)
                nc.vector.tensor_scalar(opB_lo[:, 0:8, :].rearrange("p a b -> p (a b)"), raw[:, s, :], 1.0, 0.0,
                                        ALU.is_ge, ALU.add, accum_out=full[:, bass.ds(t, 1)])\
                    .then_inc(row_full, 1)

            over_tiles(dve, row_count)
            dve.wait_ge(row_summed, TILES)
            dve.wait_ge(row_full, TILES)
            nc.vector.tensor_scalar(deg1[:, :], deg[:, :], 1.0, None, ALU.add).then_inc(degree_step, 1)
            nc.vector.tensor_scalar(count_safe[:, :], count[:, :], EDGE_EPS ** 2, None, ALU.max)\
                .then_inc(degree_step, 1)
            dve.wait_ge(pow_done, 1)
            for t in range(TILES):
                dve.wait_ge(z_hi, t // 2 * 2 + 2)
                nc.vector.scalar_tensor_tensor(opA_lo[:, t, :], xw_out(t), dinv[:, t:t + 1], f32(opA_hi[:, t, :]),
                                               ALU.mult, ALU.subtract).then_inc(z_lo, 1)
            dve.wait_ge(pow_done, 2)
            nc.vector.tensor_tensor(head_sum[:, :], count[:, :], rcount[:, :], ALU.mult).then_inc(degree_step, 1)
            dve.wait_ge(degree_step, 3)
            nc.vector.tensor_tensor(edge_deg[:, :], head_sum[:, :], deg[:, :], ALU.add).then_inc(degree_step, 1)
            dve.wait_ge(degree_step, 4)
            nc.vector.reciprocal(redge[:, :], edge_deg[:, :]).then_inc(degree_step, 1)
            dve.wait_ge(w_in, 16 * 9)
            nc.vector.tensor_scalar(diag_full[:, :], diag[:, :], 1.0, None, ALU.is_ge).then_inc(flag_step, 1)
            dve.wait_ge(flag_step, 1)
            nc.vector.tensor_tensor(diag_full[:, :], full[:, :], diag_full[:, :], ALU.subtract).then_inc(flag_step, 1)
            dve.wait_ge(flag_step, 2)
            dve.wait_ge(consts, 4)
            nc.vector.reduce_sum(sums[:, 0:1], diag_full[:, :], axis=AX.X).then_inc(flag_step, 1)

            def split_lo(L, t, s, q):
                dve.wait_ge(L["hi"], t * CHUNKS + q + 1)
                nc.vector.tensor_tensor(part_lo[:, q, :], raw[:, s, q * BLK:(q + 1) * BLK], f32(part_hi[:, q, :]),
                                        ALU.subtract).then_inc(L["lo"], 1)

            def statistics(L, u, b):
                dve.wait_ge(L["y"], u + 1)
                nc.vector.bn_stats(stats[:, b, :], ysum[:, b, :]).then_inc(L["stats"], 1)
                dve.wait_ge(L["stats"], u + 1)
                wait(dve, L["rstd"], u - 1)
                own_instruction(dve, dve_held)
                nc.vector.bn_aggr(mv[:, b, :], stats[:, b, :]).then_inc(L["mv"], 1)

            def norm(L, u, b):
                dve.wait_ge(L["rstd"], u + 1)
                wait(dve, L["rows"], u - 1)
                nc.vector.tensor_scalar(xn[:, b, :], ysum[:, b, :], mv[:, b, 0:1], rstd[:, b, :],
                                        ALU.subtract, ALU.mult).then_inc(L["xn"], 1)

            def step0(t, s):
                b, u = 1 - s, t - 1
                for q in range(CHUNKS):
                    if active(t, 0):
                        split_lo(L0, t, s, q)
                    if q == 1 and active(t, 1):
                        dve.wait_ge(L0["acc"], u + 1)
                        wait(dve, L0["y"], u)
                        nc.vector.tensor_scalar(branch[:, :], acc_weighted[b], dinv[:, bass.ds(u, 1)], 0.0,
                                                ALU.mult, ALU.max).then_inc(L0["branch"], 1)
                        dve.wait_ge(L0["branch"], u + 1)
                        nc.vector.tensor_tensor(ysum[:, b, :], branch[:, :], X[:, u, :], ALU.add)\
                            .then_inc(L0["y"], 1)
                        statistics(L0, u, b)
                if active(t, 1):
                    wait(dve, L0["op_hi"], u - 1)
                    wait(dve, L0["op_lo"], u - 1)
                    norm(L0, u, b)
                    dve.wait_ge(L0["op_hi"], u + 1)
                    nc.vector.tensor_tensor(opB_lo[:, u, :], xn[:, b, :], f32(opB_hi[:, u, :]), ALU.subtract)\
                        .then_inc(L0["op_lo"], 1)

            over_tiles(dve, step0, lag=1)

            dve.wait_ge(totals_done, 1)
            nc.vector.tensor_copy(flag[0:1, 0:4], totals).then_inc(flag_step, 1)
            dve.wait_ge(flag_step, 4)
            nc.vector.tensor_tensor(flag[0:1, 4:5], flag[0:1, 1:2], flag[0:1, 2:3], ALU.mult).then_inc(flag_step, 1)
            dve.wait_ge(flag_step, 5)
            nc.vector.tensor_scalar(flag[0:1, 5:6], flag[0:1, 4:5], NORMS_BOUND, None, ALU.is_ge)\
                .then_inc(flag_step, 1)
            dve.wait_ge(flag_step, 6)
            nc.vector.tensor_tensor(flag_int[0:1, :], flag[0:1, 0:1], flag[0:1, 5:6], ALU.add).then_inc(flag_step, 1)

            def step1(t, s):
                for q in range(CHUNKS):
                    if active(t, 0):
                        split_lo(L1, t, s, q)
                        nc.vector.tensor_scalar(edges[:, q, :], raw[:, s, q * BLK:(q + 1) * BLK], 0.0, None,
                                                ALU.is_gt).then_inc(L1["edges"], 1)
                    b, u = 1 - s, t - 1
                    if q == 1 and active(t, 1):
                        dve.wait_ge(L1["branch"], u + 1)
                        nc.vector.tensor_tensor(ysum[:, b, :], acc_weighted[b], branch[:, :], ALU.add)\
                            .then_inc(L1["sum"], 1)
                        dve.wait_ge(L1["sum"], u + 1)
                        nc.vector.scalar_tensor_tensor(ysum[:, b, :], ysum[:, b, :], redge[:, bass.ds(u, 1)],
                                                       X[:, u, :], ALU.mult, ALU.add).then_inc(L1["y"], 1)
                        statistics(L1, u, b)
                    if q == 1 and active(t, 2):
                        v = t - 2
                        dve.wait_ge(L1["value_ps"], v + 1)
                        wait(dve, L1["value_hi"], v)
                        wait(dve, L1["value_lo"], v)
                        nc.vector.tensor_tensor(vf[:, :], value_out, bv_sb[:, :], ALU.add).then_inc(L1["value"], 1)
                        for c in range(DC):
                            dve.wait_ge(L1["key_hi"], DC * v + DC)
                            nc.vector.scalar_tensor_tensor(keyT_lo[:, c, tile_cols(v)], key_out[:, c, :],
                                                           bk_sb[:, c:c + 1], f32(keyT_hi[:, c, tile_cols(v)]),
                                                           ALU.add, ALU.subtract).then_inc(L1["key_lo"], 1)
                        dve.wait_ge(L1["value_hi"], v + 1)
                        nc.vector.tensor_tensor(opA_lo[:, v, :], vf[:, :], f32(opA_hi[:, v, :]), ALU.subtract)\
                            .then_inc(L1["value_lo"], 1)
                if active(t, 1):
                    wait(dve, L1["xT_ps"], u - 1)
                    norm(L1, u, b)

            over_tiles(dve, step1, lag=2)

            def step2(t, s):
                if active(t, 4):
                    u = t - 4
                    dve.wait_ge(L2["mixed"], u + 1)
                    nc.vector.tensor_tensor(y3[:, :], mixed, xn[:, s, :], ALU.add).then_inc(L2["y3"], 1)
                    dve.wait_ge(L2["y3"], u + 1)
                    nc.vector.bn_stats(stats3[:, :], y3[:, :]).then_inc(L2["stats3"], 1)
                    dve.wait_ge(L2["stats3"], u + 1)
                    own_instruction(dve, dve_held)
                    nc.vector.bn_aggr(mv3[:, :], stats3[:, :]).then_inc(L2["mv3"], 1)
                if active(t, 3):
                    b, u = 1 - s, t - 3
                    dve.wait_ge(L2["attended"], (u + 1) * CHUNKS)
                    dve.wait_ge(L2["exp"], u + 1)
                    nc.vector.reciprocal(rsum[:, :], wsum[:, b, :]).then_inc(L2["rsum"], 1)
                    dve.wait_ge(L2["rsum"], u + 1)
                    nc.vector.scalar_tensor_tensor(ysum[:, b, :], attended, rsum[:, :], X[:, u, :],
                                                   ALU.mult, ALU.add).then_inc(L2["y"], 1)
                    statistics(L2, u, b)
                if active(t, 4):
                    u = t - 4
                    dve.wait_ge(L2["rstd3"], u + 1)
                    wait(dve, L2[f"stored{s}"], (u - s) * 8)
                    nc.vector.tensor_scalar(out_tile[:, s, :], y3[:, :], mv3[:, 0:1], rstd3[:, :],
                                            ALU.subtract, ALU.mult).then_inc(L2["out"], 1)
                if active(t, 1):
                    b, u = 1 - s, t - 1
                    dve.wait_ge(L2[f"in{b}"], loaded(u, b))
                    wait(dve, L2["mx"], u)
                    for q in range(CHUNKS):
                        dve.wait_ge(L2["scores"], (u * CHUNKS) + q + 1)
                        own_instruction(dve, dve_held)
                        part = raw[:, b, q * BLK:(q + 1) * BLK]
                        nc.vector.tensor_tensor_reduce(out=part, in0=wide[:, q, :], in1=part, scale=2.0,
                                                       scalar=LOWEST, op0=ALU.add, op1=ALU.max,
                                                       accum_out=mx[:, q:q + 1]).then_inc(L2["masked"], 1)
                        if q == 1 and active(t, 3):
                            norm(L2, t - 3, b)
                    dve.wait_ge(L2["masked"], (u + 1) * CHUNKS)
                    wait(dve, L2["exp"], u - 1)
                    nc.vector.reduce_max(nmax[:, b, :], mx[:, :], axis=AX.X).then_inc(L2["mx"], 1)
                    dve.wait_ge(L2["mx"], u + 1)
                    nc.vector.tensor_scalar(nmax[:, b, :], nmax[:, b, :], -1.0, None, ALU.mult)\
                        .then_inc(L2["nmax"], 1)
                elif active(t, 3):
                    norm(L2, t - 3, 1 - s)
                if active(t, 0):
                    dve.wait_ge(L2["q_ps"], t + 1)
                    wait(dve, L2["q_hi"], t)
                    wait(dve, L2["q_lo"], t)
                    for c in range(DC):
                        nc.vector.tensor_scalar(qf[:, c, :], q_out[:, c, :], bq_sb[:, c:c + 1], ATT_SCALE / 2,
                                                ALU.add, ALU.mult).then_inc(L2["qf"], 1)
                    dve.wait_ge(L2["q_hi"], t + 1)
                    nc.vector.tensor_tensor(q_lo[:, :, :], qf[:, :, :], f32(q_hi[:, :, :]), ALU.subtract)\
                        .then_inc(L2["q_lo"], 1)
                if active(t, 2):
                    u = t - 2
                    for q in range(CHUNKS):
                        dve.wait_ge(L2["w_hi"], u * CHUNKS + q + 1)
                        nc.vector.tensor_tensor(part_lo[:, q, :], bank[q % 2][:, :], f32(part_hi[:, q, :]),
                                                ALU.subtract).then_inc(L2["w_lo"], 1)

            over_tiles(dve, step2, lag=4, peel=4)

            with dve.If(needed(dve)):
                dve.wait_ge(L2["out"], TILES)
                dve.wait_ge(L2["xT_all"], TILES)
                dve.wait_ge(L2["stored0"], 16 * TILES // 2)
                dve.wait_ge(L2["stored1"], 16 * TILES // 2)
                nc.vector.memset(head_padded[:, :], 0.0).then_inc(G["zeroed"], 1)
                dve.wait_ge(G["zeroed"], 1)
                nc.vector.memset(mx[:, :], 0.0).then_inc(G["taken"], 1)
                dve.wait_ge(G["taken"], 1)
                nc.vector.memset(mx[:, :], 0.0).then_inc(G["added"], 1)

                def head_operands(h):
                    dve.wait_ge(G["key_hi"], h + 1)
                    nc.vector.tensor_tensor(head_key_lo, head_key_out.rearrange("p q n -> p (q n)"), f32(head_key_hi),
                                            ALU.subtract).then_inc(G["key_lo"], 1)
                    dve.wait_ge(G["value_hi"], h * 2 + 2)
                    for k in range(2):
                        part = slice(k * TILES // 2, (k + 1) * TILES // 2)
                        nc.vector.tensor_tensor(head_value_lo[:, part, :], head_value_out[k],
                                                f32(head_value_hi[:, part, :]), ALU.subtract)\
                            .then_inc(G["value_lo"], 1)

                def tile(n, t):
                    dve.wait_ge(G["q_ps"], n + 1)
                    nc.vector.tensor_scalar(head_qf, head_q_out, HEAD_SCALE, None, ALU.mult).then_inc(G["qf"], 1)
                    dve.wait_ge(G["q_hi"], n + 1)
                    nc.vector.tensor_tensor(head_q_lo, head_qf, f32(head_q_hi), ALU.subtract).then_inc(G["q_lo"], 1)
                    dve.wait_ge(G["adj_in"], n * 16 + 16)
                    on_diagonal = adj_sb[:, tile_cols(t)]
                    nc.vector.tensor_tensor(on_diagonal, on_diagonal, ident[:, :], ALU.max).then_inc(G["penalty"], 1)
                    dve.wait_ge(G["penalty"], 2 * n + 1)
                    nc.vector.tensor_scalar(adj_sb, adj_sb, -1.0, 1.0, ALU.mult, ALU.add).then_inc(G["penalty"], 1)
                    dve.wait_ge(G["scores"], n + 1)
                    dve.wait_ge(G["penalty"], 2 * n + 2)
                    nc.vector.scalar_tensor_tensor(scores_sb, adj_sb, -MASK_VAL, wide[:, :, :].rearrange("p q n -> p (q n)"),
                                                   ALU.mult, ALU.add).then_inc(G["taken"], 1)
                    dve.wait_ge(G["taken"], n + 2)
                    on_diagonal = scores_sb[:, tile_cols(t)]
                    nc.vector.scalar_tensor_tensor(on_diagonal, ident[:, :], IDENTITY_BIAS, on_diagonal,
                                                   ALU.mult, ALU.add).then_inc(G["masked"], 1)
                    dve.wait_ge(G["masked"], n + 1)
                    nc.vector.reduce_max(nmax[:, 1, :], scores_sb, axis=AX.X).then_inc(G["mx"], 1)
                    dve.wait_ge(G["mx"], 2 * n + 1)
                    nc.vector.tensor_scalar(nmax[:, 0, :], nmax[:, 1, :], -1.0, None, ALU.mult).then_inc(G["mx"], 1)
                    for q in range(CHUNKS):
                        dve.wait_ge(G["w_hi"], n * CHUNKS + q + 1)
                        nc.vector.tensor_tensor(part_lo[:, q, :], bank[q % 2][:, :], f32(part_hi[:, q, :]),
                                                ALU.subtract).then_inc(G["w_lo"], 1)
                    dve.wait_ge(G["exp"], n + 1)
                    nc.vector.reciprocal(rsum[:, :], wsum[:, 0, :]).then_inc(G["rsum"], 1)
                    dve.wait_ge(G["attended"], n + 1)
                    dve.wait_ge(G["rsum"], n + 1)
                    nc.vector.tensor_scalar(head_padded[:, 0:KD], head_attended, rsum[:, :], None, ALU.mult)\
                        .then_inc(G["head"], 1)
                    dve.wait_ge(G["mixed"], n + 1)
                    nc.vector.tensor_tensor(X[:, t, :], X[:, t, :], head_mixed, ALU.add).then_inc(G["added"], 1)

                heads_and_tiles(dve, head_operands, tile)
                dve.wait_ge(G["added"], HEADS * TILES + 1)
                for s in range(2):
                    dve.sem_inc(G[f"stored{s}"], 16)
                with dve.Fori(0, TILES // 2) as pair:
                    for s in range(2):
                        t = pair * 2 + s
                        nc.vector.bn_stats(stats3[:, :], X[:, t, :]).then_inc(G["stats"], 1)
                        dve.wait_ge(G["stats"], t + 1)
                        own_instruction(dve, dve_held)
                        nc.vector.bn_aggr(mv3[:, :], stats3[:, :]).then_inc(G["mv"], 1)
                        dve.wait_ge(G["rstd"], t + 1)
                        dve.wait_ge(G[f"stored{s}"], pair * 16 + 16)
                        nc.vector.tensor_scalar(out_tile[:, s, :], X[:, t, :], mv3[:, 0:1], rstd3[:, :],
                                                ALU.subtract, ALU.mult).then_inc(G["normed"], 1)

        @block.tensor
        def _(pe):
            pe.wait_ge(stage_vo_in, 32)
            for c in range(DC):
                for k in range(HK // P):
                    last = nc.tensor.matmul(wvo_out[c], stage[:, 0, k * D + c * P:k * D + (c + 1) * P],
                                            stage[:, 1, k * D:(k + 1) * D], start=k == 0, stop=k == HK // P - 1)
            last.then_inc(wvo_ps, 1)
            pe.wait_ge(xT_in, 32)
            for t in range(TILES):
                if t == TILES - 2:
                    pe.wait_ge(wvo_ready, DC)
                for c in range(DC):
                    last = nc.tensor.matmul(xw_out(t), XT[:, c, t * P:(t + 1) * P], w0_sb[:, c, :],
                                            start=c == 0, stop=c == DC - 1)
                last.then_inc(xw_done, 1)
            pe.wait_ge(flag_step, 3)
            pe.wait_ge(norms_done, 2)
            pe.wait_ge(z_lo, TILES)
            nc.tensor.matmul(totals, ones[:, 0:1], sums[:, :], start=True, stop=True).then_inc(totals_done, 1)
            pe.wait_ge(ident_ready, 1)

            def weighted_sum(L, t, s, q, op_hi, op_lo, last_tile_stop):
                pe.wait_ge(L["lo"], t * CHUNKS + q + 1)
                if L is L1:
                    pe.wait_ge(L1["edges"], t * CHUNKS + q + 1)
                for k in range(SUB):
                    j = q * SUB + k
                    hi, lo, edge = (part[:, q, k * P:(k + 1) * P] for part in (part_hi, part_lo, edges))
                    first, end = j == 0, j == TILES - 1
                    nc.tensor.matmul(acc_weighted[s], hi, op_hi[:, j, :], start=first, stop=False)
                    nc.tensor.matmul(acc_weighted[s], hi, op_lo[:, j, :], start=False, stop=False)
                    last = nc.tensor.matmul(acc_weighted[s], lo, op_hi[:, j, :], start=False,
                                            stop=end and last_tile_stop)
                    if L is L1:
                        nc.tensor.matmul(acc_edges[s], edge, op_hi[:, j, :], start=first, stop=False)
                        last = nc.tensor.matmul(acc_edges[s], edge, op_lo[:, j, :], start=False, stop=end)
                last.then_inc(L["chunk_used"], 1)

            def step0(t, s):
                wait(pe, L0["branch"], t - 1)
                for q in range(CHUNKS):
                    weighted_sum(L0, t, s, q, opA_hi, opA_lo, False)
                nc.tensor.matmul(acc_weighted[s], ident_r[:, :], opA_hi[:, t, :], start=False, stop=False)
                nc.tensor.matmul(acc_weighted[s], ident_r[:, :], opA_lo[:, t, :], start=False, stop=True)\
                    .then_inc(L0["acc"], 1)

            over_tiles(pe, step0)

            pe.wait_ge(L0["op_lo"], TILES)
            pe.wait_ge(L0["branch"], TILES)

            def step1(t, s):
                for q in range(CHUNKS):
                    if active(t, 0):
                        if q == 0:
                            wait(pe, L1["sum"], t - 1)
                        weighted_sum(L1, t, s, q, opB_hi, opB_lo, True)
                    if q == 0 and active(t, 2):
                        v = t - 2
                        pe.wait_ge(L1["xT"], v + 1)
                        wait(pe, L1["key_lo"], DC * v)
                        wait(pe, L1["value"], v)
                        for o in range(DC):
                            for c in range(DC):
                                last = nc.tensor.matmul(key_out[:, o, :], wkT_sb[:, c, o * P:(o + 1) * P],
                                                        xT_tile[:, s, c, :], start=c == 0, stop=c == DC - 1)
                        last.then_inc(L1["key_ps"], 1)
                        for c in range(DC):
                            last = nc.tensor.matmul(value_out, xT_tile[:, s, c, :], wvT_sb[:, c, :],
                                                    start=c == 0, stop=c == DC - 1)
                        last.then_inc(L1["value_ps"], 1)
                if active(t, 1):
                    u = t - 1
                    pe.wait_ge(L1["xn"], u + 1)
                    wait(pe, L1["xT"], u)
                    for c in range(DC):
                        last = nc.tensor.transpose(xT_out1[:, c, :], xn[:, 1 - s, c * P:(c + 1) * P], ident[:, :])
                    last.then_inc(L1["xT_ps"], 1)

            over_tiles(pe, step1, lag=2)
            pe.wait_ge(L1["key_lo"], DC * TILES)
            pe.wait_ge(L1["value_lo"], TILES)
            pe.wait_ge(L1["xT_all"], TILES)

            def step2(t, s):
                if active(t, 1):
                    u = t - 1
                    pe.wait_ge(L2["q_lo"], u + 1)
                    for q in range(CHUNKS):
                        wait(pe, L2["masked"], (u - 1) * CHUNKS + q + 1)
                        for c in range(DC):
                            keys = slice(q * BLK, (q + 1) * BLK)
                            nc.tensor.matmul(wide[:, q, :], q_hi[:, c, :], keyT_hi[:, c, keys], start=c == 0, stop=False)
                            nc.tensor.matmul(wide[:, q, :], q_hi[:, c, :], keyT_lo[:, c, keys], start=False, stop=False)
                            last = nc.tensor.matmul(wide[:, q, :], q_lo[:, c, :], keyT_hi[:, c, keys],
                                                    start=False, stop=c == DC - 1)
                        last.then_inc(L2["scores"], 1)
                if active(t, 3):
                    u = t - 3
                    pe.wait_ge(L2["xn"], u + 1)
                    wait(pe, L2["xT"], u)
                    pe.wait_ge(L2["qf"], DC * t if active(t, 0) else DC * TILES)
                    for c in range(DC):
                        last = nc.tensor.transpose(xT_out2[:, c, :], xn[:, 1 - s, c * P:(c + 1) * P], ident[:, :])
                    last.then_inc(L2["xT_ps"], 1)
                if active(t, 0):
                    wait(pe, L2["qf"], DC * t)
                    if active(t, 4):
                        pe.wait_ge(L2["xT"], t - 3)
                    for o in range(DC):
                        for c in range(DC):
                            last = nc.tensor.matmul(q_out[:, o, :], wqT_sb[:, c, o * P:(o + 1) * P],
                                                    XT[:, c, tile_cols(t)], start=c == 0, stop=c == DC - 1)
                    last.then_inc(L2["q_ps"], 1)
                if active(t, 2):
                    u = t - 2

                    def transpose_weights(q):
                        if q == 0:
                            pe.wait_ge(L2["exp"], u + 1)
                        wait(pe, L2["w_lo"], u * CHUNKS + q - 1)
                        for k in range(SUB):
                            j = q * SUB + k
                            last = nc.tensor.transpose(bank[q % 2][:, k * P:(k + 1) * P],
                                                       raw[:, s, j * P:(j + 1) * P], ident[:, :])
                        last.then_inc(L2["tr_ps"], 1)

                    def attend(q):
                        if q == 0:
                            wait(pe, L2["y"], u)
                            wait(pe, L2["y3"], u - 1)
                        pe.wait_ge(L2["w_lo"], u * CHUNKS + q + 1)
                        for k in range(SUB):
                            j = q * SUB + k
                            hi, lo = (part[:, q, k * P:(k + 1) * P] for part in (part_hi, part_lo))
                            nc.tensor.matmul(attended, hi, opA_hi[:, j, :], start=j == 0, stop=False)
                            nc.tensor.matmul(attended, hi, opA_lo[:, j, :], start=False, stop=False)
                            last = nc.tensor.matmul(attended, lo, opA_hi[:, j, :], start=False, stop=j == TILES - 1)
                        last.then_inc(L2["attended"], 1)

                    transpose_weights(0)
                    transpose_weights(1)
                    attend(0)
                    transpose_weights(2)
                    attend(1)
                    transpose_weights(3)
                    attend(2)
                    attend(3)
                if active(t, 3):
                    u = t - 3
                    pe.wait_ge(L2["xT"], u + 1)
                    wait(pe, L2["y3"], u)
                    pe.wait_ge(L2["y"], u + 1)
                    for c in range(DC):
                        last = nc.tensor.matmul(mixed, xT_tile[:, 1 - s, c, :], wvo_sb[:, c, :],
                                                start=c == 0, stop=c == DC - 1)
                    last.then_inc(L2["mixed"], 1)

            over_tiles(pe, step2, lag=3, peel=4)

            with pe.If(needed(pe)):
                def head_operands(h):
                    pe.wait_ge(G["added"], h * TILES + 1)
                    pe.wait_ge(G["weights"], h * 64 + 64)
                    for q in range(CHUNKS):
                        for c in range(DC):
                            last = nc.tensor.matmul(head_key_out[:, q, :], head_wk[:, c, :],
                                                    XT[:, c, q * BLK:(q + 1) * BLK], start=c == 0, stop=c == DC - 1)
                    last.then_inc(G["key_ps"], 1)
                    for j in range(TILES):
                        for c in range(DC):
                            last = nc.tensor.matmul(head_value_out[j // 8][:, j % 8, :], XT[:, c, j * P:(j + 1) * P],
                                                    head_wv[:, c, :], start=c == 0, stop=c == DC - 1)
                    last.then_inc(G["value_ps"], 1)
                    pe.wait_ge(G["key_lo"], h + 1)
                    pe.wait_ge(G["value_lo"], h * 2 + 2)
                    own_instruction(pe, pe_held)

                def tile(n, t):
                    pe.wait_ge(G["added"], n + 1)
                    for c in range(DC):
                        last = nc.tensor.matmul(head_q_out, head_wq[:, c, :], XT[:, c, tile_cols(t)],
                                                start=c == 0, stop=c == DC - 1)
                    last.then_inc(G["q_ps"], 1)
                    pe.wait_ge(G["q_lo"], n + 1)
                    for q in range(CHUNKS):
                        keys = slice(q * BLK, (q + 1) * BLK)
                        nc.tensor.matmul(wide[:, q, :], head_q_hi, head_key_hi[:, keys], start=True, stop=False)
                        nc.tensor.matmul(wide[:, q, :], head_q_hi, head_key_lo[:, keys], start=False, stop=False)
                        last = nc.tensor.matmul(wide[:, q, :], head_q_lo, head_key_hi[:, keys], start=False, stop=True)
                    last.then_inc(G["scores"], 1)
                    pe.wait_ge(G["exp"], n + 1)
                    for q in range(CHUNKS):
                        if q >= 2:
                            pe.wait_ge(G["w_lo"], n * CHUNKS + q - 1)
                        for k in range(SUB):
                            j = q * SUB + k
                            last = nc.tensor.transpose(bank[q % 2][:, k * P:(k + 1) * P],
                                                       scores_sb[:, j * P:(j + 1) * P], ident[:, :])
                        last.then_inc(G["tr_ps"], 1)
                    for q in range(CHUNKS):
                        pe.wait_ge(G["w_lo"], n * CHUNKS + q + 1)
                        for k in range(SUB):
                            j = q * SUB + k
                            hi, lo = (part[:, q, k * P:(k + 1) * P] for part in (part_hi, part_lo))
                            nc.tensor.matmul(head_attended, hi, head_value_hi[:, j, :], start=j == 0, stop=False)
                            nc.tensor.matmul(head_attended, hi, head_value_lo[:, j, :], start=False, stop=False)
                            last = nc.tensor.matmul(head_attended, lo, head_value_hi[:, j, :], start=False,
                                                    stop=j == TILES - 1)
                    last.then_inc(G["attended"], 1)
                    pe.wait_ge(G["head"], n + 1)
                    nc.tensor.transpose(head_T_out, head_padded, ident[:, :]).then_inc(G["head_t_ps"], 1)
                    pe.wait_ge(G["head_t"], n + 1)
                    nc.tensor.matmul(head_mixed, head_T[0:KD, :], head_wo, start=True, stop=True)\
                        .then_inc(G["mixed"], 1)

                heads_and_tiles(pe, head_operands, tile)


def kernel(x, adj, L0_gnn_weight, L2_gnn_Wq, L2_gnn_bq, L2_gnn_Wk, L2_gnn_bk, L2_gnn_Wv, L2_gnn_bv,
           L3_gnn_Wks, L3_gnn_Wqs, L3_gnn_Wvs, L3_gnn_Wo):
    import numpy as np
    import concourse.bacc as bacc
    from concourse.bass_utils import run_bass_kernel_spmd

    x, adj = np.asarray(x), np.asarray(adj)

    def chunked(w):
        w = np.asarray(w)
        return w.reshape(-1, P, w.shape[1]).transpose(1, 0, 2)

    def heads_side_by_side(w):
        return np.asarray(w).transpose(1, 0, 2).reshape(D, HK)

    arrays = dict(
        x=x.reshape(TILES, P, D).transpose(1, 0, 2),
        xT=chunked(x.T),
        adj=adj,
        adjT=adj.reshape(TILES, P, TILES, P).transpose(0, 3, 2, 1).reshape(N, N),
        adj_diag=np.diagonal(adj).reshape(TILES, P).T,
        w0=chunked(L0_gnn_weight),
        wqT=chunked(np.asarray(L2_gnn_Wq).T), bq=np.asarray(L2_gnn_bq).reshape(DC, P).T,
        wkT=chunked(np.asarray(L2_gnn_Wk).T), bk=np.asarray(L2_gnn_bk).reshape(DC, P).T,
        wvT=chunked(np.asarray(L2_gnn_Wv).T), bv=np.broadcast_to(np.asarray(L2_gnn_bv), (P, D)),
        hwk=chunked(heads_side_by_side(L3_gnn_Wks)).reshape(P, -1),
        hwq=chunked(heads_side_by_side(L3_gnn_Wqs)).reshape(P, -1),
        hwv=chunked(heads_side_by_side(L3_gnn_Wvs)).reshape(P, -1),
        hwvT=chunked(heads_side_by_side(L3_gnn_Wvs).T).reshape(P, -1),
        hwo=chunked(np.asarray(L3_gnn_Wo).reshape(HK, D)).reshape(P, -1),
        hwo_rows=np.asarray(L3_gnn_Wo).reshape(HK, D),
        ident_in=np.eye(P, dtype=np.float32),
    )
    nc = bacc.Bacc("TRN2", target_bir_lowering=False, num_devices=1)
    arrays = {name: np.ascontiguousarray(a) for name, a in arrays.items()}
    args = {name: nc.dram_tensor(f"{name}_dram", a.shape, mybir.dt.from_np(a.dtype), kind="ExternalInput").ap()
            for name, a in arrays.items()}
    out = nc.dram_tensor("out_dram", (N, D), F32, kind="ExternalOutput").ap()
    build(nc, out=out, **args)
    r = run_bass_kernel_spmd(nc, [{f"{name}_dram": a for name, a in arrays.items()}], core_ids=[0])
    return r.results[0]["out_dram"]
```

```python
import concourse.bass as bass
from concourse import mybir
from contextlib import ExitStack

F32 = mybir.dt.float32
F32R = mybir.dt.float32r
I32 = mybir.dt.int32
ALU = mybir.AluOpType
ACT = mybir.ActivationFunctionType
AX = mybir.AxisListType

P = 128
N = 2048
D = 256
TILES = N // P
DC = D // P
BLK = 512
CHUNKS = N // BLK
SUB = BLK // P
HEADS = 8
KD = 64
HK = HEADS * KD
LN_EPS = 1e-5
EDGE_EPS = 1e-12
ATT_SCALE = float(D) ** -0.5
HEAD_SCALE = float(KD) ** -0.5
IDENTITY_BIAS = 0.01
MASK_VAL = 1e16
LOWEST = -3.0e38
FLAG_STEPS = 10
NORMS_BOUND = (1e8 / (D * HEAD_SCALE)) ** 2


def active(t, lag, count=TILES):
    return not isinstance(t, int) or lag <= t < count + lag


def wait(eng, sem, value):
    if not isinstance(value, int) or value > 0:
        eng.wait_ge(sem, value)


def own_instruction(eng, held):
    eng.sem_inc(held, 1)


def over_tiles(eng, step, lag=0, count=TILES, peel=2):
    for t in range(peel):
        step(t, t % 2)
    with eng.Fori(peel // 2, count // 2) as pair:
        step(pair * 2, 0)
        step(pair * 2 + 1, 1)
    for t in range(count, count + lag):
        step(t, t % 2)


def loaded(t, s):
    return (t - s) * 8 + 16


def tile_cols(t):
    return bass.ds(t * P, P)


def f32(ap):
    return ap.bitcast(F32)


def build(nc, x, xT, adj, adjT, adj_diag, w0, wqT, bq, wkT, bk, wvT, bv, hwk, hwq, hwv, hwvT, hwo, hwo_rows, ident_in, out):
    with ExitStack() as ctx:
        def sb(name, shape, dt=F32):
            return ctx.enter_context(nc.sbuf_tensor(name, shape, dt))

        def sem(name):
            return ctx.enter_context(nc.semaphore(name))

        X = sb("X", [P, TILES, D])
        XT = sb("XT", [P, DC, N])
        opA_hi = sb("opA_hi", [P, TILES, D], F32R)
        opA_lo = sb("opA_lo", [P, TILES, D], F32R)
        opB_hi = sb("opB_hi", [P, TILES, D], F32R)
        opB_lo = sb("opB_lo", [P, TILES, D], F32R)
        keyT_hi = sb("keyT_hi", [P, DC, N], F32R)
        keyT_lo = sb("keyT_lo", [P, DC, N], F32R)
        raw = sb("raw", [P, 2, N])
        part_hi = sb("part_hi", [P, CHUNKS, BLK], F32R)
        part_lo = sb("part_lo", [P, CHUNKS, BLK], F32R)
        edges = sb("edges", [P, CHUNKS, BLK], F32R)
        w0_sb = sb("w0_sb", [P, DC, D])
        wqT_sb = sb("wqT_sb", [P, DC, D])
        wkT_sb = sb("wkT_sb", [P, DC, D])
        wvT_sb = sb("wvT_sb", [P, DC, D])
        bq_sb = sb("bq_sb", [P, DC])
        bk_sb = sb("bk_sb", [P, DC])
        bv_sb = sb("bv_sb", [P, D])
        stage = sb("stage", [P, 2, HK * D // P])
        wvo_sb = sb("wvo_sb", [P, DC, D])
        ident = sb("ident", [P, P])
        ident_r = sb("ident_r", [P, P], F32R)
        ones = sb("ones", [P, P])
        deg = sb("deg", [P, TILES])
        count = sb("count", [P, TILES])
        sign_out = sb("sign_out", [P, N], mybir.dt.bfloat16)
        signs = sb("signs", [P, TILES])
        below_one = sb("below_one", [P, 1])
        diag = sb("diag", [P, TILES])
        diag_sign = sb("diag_sign", [P, TILES])
        diag_least = sb("diag_least", [P, TILES])
        deg1 = sb("deg1", [P, TILES])
        count_safe = sb("count_safe", [P, TILES])
        head_sum = sb("head_sum", [P, TILES])
        edge_deg = sb("edge_deg", [P, TILES])
        dinv = sb("dinv", [P, TILES])
        rcount = sb("rcount", [P, TILES])
        redge = sb("redge", [P, TILES])
        minus_half = sb("minus_half", [P, TILES])
        ln_eps = sb("ln_eps", [P, 1])
        sums = sb("sums", [P, 4])
        flag = sb("flag", [1, 8])
        flag_int = sb("flag_int", [1, 1], I32)
        branch = sb("branch", [P, D])
        ysum = sb("ysum", [P, 2, D])
        xn = sb("xn", [P, 2, D])
        stats = sb("stats", [P, 2, 6])
        mv = sb("mv", [P, 2, 2])
        veps = sb("veps", [P, 2, 1])
        rstd = sb("rstd", [P, 2, 1])
        xT_tile = sb("xT_tile", [P, 2, DC, P])
        vf = sb("vf", [P, D])
        qf = sb("qf", [P, DC, P])
        q_hi = sb("q_hi", [P, DC, P], F32R)
        q_lo = sb("q_lo", [P, DC, P], F32R)
        mx = sb("mx", [P, CHUNKS])
        nmax = sb("nmax", [P, 2, 1])
        wsum = sb("wsum", [P, 2, 1])
        rsum = sb("rsum", [P, 1])
        y3 = vf
        stats3 = sb("stats3", [P, 6])
        mv3 = sb("mv3", [P, 2])
        veps3 = sb("veps3", [P, 1])
        rstd3 = sb("rstd3", [P, 1])
        out_tile = sb("out_tile", [P, 2, D])

        wide = ctx.enter_context(nc.psum_tensor("wide", [P, CHUNKS, BLK], F32))
        bank = [ctx.enter_context(nc.psum_tensor(f"bank{i}", [P, BLK], F32)) for i in range(4)]

        def xw_out(t):
            half = slice((t % 2) * D, (t % 2 + 1) * D)
            return wide[:, t // 2, half] if t < 8 else bank[t // 2 - 4][:, half]

        wvo_out = [bank[3][:, c * D:(c + 1) * D] for c in range(DC)]
        totals = bank[2][0:1, 0:4]
        acc_weighted = [wide[:, s, 0:D] for s in range(2)]
        acc_edges = [wide[:, 2 + s, 0:D] for s in range(2)]
        xT_out1 = bank[0][:, 0:D].rearrange("p (c q) -> p c q", c=DC)
        key_out = bank[1][:, 0:D].rearrange("p (c q) -> p c q", c=DC)
        value_out = bank[2][:, 0:D]
        q_out = bank[3][:, 0:D].rearrange("p (c q) -> p c q", c=DC)
        xT_out2 = bank[3][:, D:2 * D].rearrange("p (c q) -> p c q", c=DC)
        attended = bank[2][:, 0:D]
        mixed = bank[2][:, D:2 * D]

        xT_in, w_in, stage_vo_in, stage_qk_in = (sem(n) for n in ("xT_in", "w_in", "stage_vo_in", "stage_qk_in"))
        row_in = [sem(f"row_in{s}") for s in range(2)]
        row_summed, row_counted = sem("row_summed"), sem("row_counted")
        dve_held, pe_held = sem("dve_held"), sem("pe_held")
        consts, ident_ready = sem("consts"), sem("ident_ready")
        xw_done, wvo_ps, wvo_ready = sem("xw_done"), sem("wvo_ps"), sem("wvo_ready")
        norms_done, degree_step, flag_step = sem("norms_done"), sem("degree_step"), sem("flag_step")
        pow_done, z_hi, z_lo, totals_done = sem("pow_done"), sem("z_hi"), sem("z_lo"), sem("totals_done")

        def named(prefix, names):
            return {n: sem(f"{prefix}_{n}") for n in names.split()}

        L0 = named("l0", "in0 in1 hi lo chunk_used acc branch y stats mv veps rstd xn rows op_hi op_lo")
        L1 = named("l1", "in0 in1 hi lo edges chunk_used branch sum y stats mv veps rstd xn rows "
                         "signs xT_ps xT xT_all key_ps key_hi key_lo value_ps value value_hi value_lo")
        L2 = named("l2", "in0 in1 q_ps qf q_hi q_lo scores masked mx nmax exp tr_ps w_hi w_lo attended "
                         "rsum y stats mv veps rstd xn rows xT_ps xT xT_all mixed "
                         "y3 stats3 mv3 veps3 rstd3 out stored0 stored1")

        G = named("l3", "weights key_ps key_hi key_lo value_ps value_hi value_lo adj_in q_ps qf q_hi q_lo "
                        "scores penalty taken masked mx exp tr_ps w_hi w_lo attended rsum head head_t_ps head_t mixed "
                        "added stats mv veps rstd normed stored0 stored1 zeroed")

        head_wq, head_wk, head_wv = (stage[:, 0, k * DC * KD:(k + 1) * DC * KD].rearrange("p (c k) -> p c k", c=DC)
                                     for k in range(3))
        head_wo = stage[0:KD, 1, 0:D]
        head_key_hi, head_key_lo = keyT_hi[0:KD, 0, :], keyT_lo[0:KD, 0, :]
        head_value_hi, head_value_lo = opA_hi[:, :, 0:KD], opA_lo[:, :, 0:KD]
        head_qf, head_q_hi, head_q_lo = qf[0:KD, 0, :], q_hi[0:KD, 0, :], q_lo[0:KD, 0, :]
        head_key_out = wide[0:KD, :, :]
        head_value_out = [bank[2 + k][:, :].rearrange("p (t k) -> p t k", t=TILES // 2) for k in range(2)]
        head_q_out = bank[3][0:KD, 0:P]
        head_attended = bank[2][:, 0:KD]
        head_padded = vf[:, 0:P]
        head_T_out, head_T = bank[3][:, 0:P], qf[:, 1, :]
        head_mixed = bank[2][:, 0:D]
        scores_sb, adj_sb = raw[:, 0, :], raw[:, 1, :]

        def needed(eng):
            eng.wait_ge(flag_step, FLAG_STEPS)
            return eng.value_load(flag_int[0:1, 0:1], min_val=0, max_val=2 * N * N + 1) >= 1

        def heads_and_tiles(eng, per_head, per_tile):
            with eng.Fori(0, HEADS) as h:
                per_head(h)
                with eng.Fori(0, TILES) as t:
                    per_tile(h * TILES + t, t)

        block = ctx.enter_context(nc.Block())

        @block.sync
        def _(sp):
            def rows(t, s):
                wait(sp, row_summed, t - 1)
                wait(sp, row_counted, t - 1)
                sp.dma_start(raw[:, s, :], adj[tile_cols(t), :]).then_inc(row_in[s], 16)

            over_tiles(sp, rows)

            def blocks0(t, s):
                if isinstance(t, int) and t < 2:
                    sp.wait_ge(row_summed, TILES - 1 + t)
                    sp.wait_ge(row_counted, TILES - 1 + t)
                wait(sp, L0["lo"], (t - 1) * CHUNKS)
                sp.dma_start(raw[:, s, :], adjT[tile_cols(t), :]).then_inc(L0[f"in{s}"], 16)

            over_tiles(sp, blocks0)

            def blocks1(t, s):
                if isinstance(t, int) and t < 2:
                    sp.wait_ge(L0["lo"], (TILES - 1 + t) * CHUNKS)
                wait(sp, L1["lo"], (t - 1) * CHUNKS)
                wait(sp, L1["edges"], (t - 1) * CHUNKS)
                wait(sp, L1["signs"], t - 1)
                sp.dma_start(raw[:, s, :], adjT[tile_cols(t), :]).then_inc(L1[f"in{s}"], 16)

            over_tiles(sp, blocks1)

            def attention(t, s):
                if active(t, 4):
                    u = t - 4
                    sp.wait_ge(L2["out"], u + 1)
                    sp.dma_start(out[tile_cols(u), :], out_tile[:, s, :]).then_inc(L2[f"stored{s}"], 16)
                if active(t, 0):
                    if isinstance(t, int) and t < 2:
                        sp.wait_ge(L1["lo"], (TILES - 1 + t) * CHUNKS)
                        sp.wait_ge(L1["edges"], (TILES - 1 + t) * CHUNKS)
                    wait(sp, L2["tr_ps"], (t - 1) * CHUNKS)
                    sp.dma_start(raw[:, s, :], adj[tile_cols(t), :]).then_inc(L2[f"in{s}"], 16)

            over_tiles(sp, attention, lag=4, peel=4)
            for s in range(2):
                sp.wait_ge(L2[f"stored{s}"], 16 * TILES // 2)

            with sp.If(needed(sp)):
                def weights(h):
                    sp.wait_ge(G["added"], h * TILES + 1)
                    for dst, src in ((head_wq, hwq), (head_wk, hwk), (head_wv, hwv)):
                        sp.dma_start(dst, src.rearrange("p (c h k) -> p c h k", c=DC, h=HEADS)[:, :, h, :])\
                            .then_inc(G["weights"], 16)
                    sp.dma_start(head_wo, hwo_rows[bass.ds(h * KD, KD), :]).then_inc(G["weights"], 16)

                def adjacency(n, t):
                    sp.wait_ge(G["taken"], n + 1)
                    sp.dma_start(adj_sb, adj[tile_cols(t), :]).then_inc(G["adj_in"], 16)

                heads_and_tiles(sp, weights, adjacency)
                with sp.Fori(0, TILES // 2) as pair:
                    for s in range(2):
                        sp.wait_ge(G["normed"], pair * 2 + s + 1)
                        sp.dma_start(out[tile_cols(pair * 2 + s), :], out_tile[:, s, :])\
                            .then_inc(G[f"stored{s}"], 16)
                for s in range(2):
                    sp.wait_ge(G[f"stored{s}"], 16 * TILES // 2 + 16)

        @block.gpsimd
        def _(pool):
            nc.gpsimd.memset(minus_half[:, :], -0.5).then_inc(consts, 1)
            nc.gpsimd.memset(ones[:, :], 1.0).then_inc(consts, 1)
            nc.gpsimd.memset(sums[:, :], 0.0).then_inc(consts, 1)
            nc.gpsimd.memset(ln_eps[:, :], LN_EPS).then_inc(consts, 1)
            nc.gpsimd.memset(below_one[:, :], -(1.0 - 2.0 ** -24)).then_inc(consts, 1)
            pool.wait_ge(consts, 5)
            pool.wait_ge(degree_step, 2)
            nc.gpsimd.tensor_tensor(dinv[:, :], deg1[:, :], minus_half[:, :], ALU.pow).then_inc(pow_done, 1)
            nc.gpsimd.tensor_tensor(rcount[:, :], count_safe[:, :], minus_half[:, :], ALU.pow).then_inc(pow_done, 1)

            def norm_scale(L, t, s):
                pool.wait_ge(L["mv"], t + 1)
                nc.gpsimd.tensor_tensor(veps[:, s, :], mv[:, s, 1:2], ln_eps[:, :], ALU.add).then_inc(L["veps"], 1)
                pool.wait_ge(L["veps"], t + 1)
                nc.gpsimd.tensor_tensor(rstd[:, s, :], veps[:, s, :], minus_half[:, 0:1], ALU.pow)\
                    .then_inc(L["rstd"], 1)

            def keep_rows(L, t, s):
                pool.wait_ge(L["xn"], t + 1)
                nc.gpsimd.tensor_copy(X[:, t, :], xn[:, s, :]).then_inc(L["rows"], 1)

            def step0(t, s):
                norm_scale(L0, t, s)
                keep_rows(L0, t, s)

            over_tiles(pool, step0)

            def step1(t, s):
                norm_scale(L1, t, s)
                keep_rows(L1, t, s)
                pool.wait_ge(L1["xT"], t + 1)
                nc.gpsimd.tensor_copy(XT[:, :, tile_cols(t)], xT_tile[:, s, :, :]).then_inc(L1["xT_all"], 1)

            over_tiles(pool, step1)

            def step2(t, s):
                if active(t, 1):
                    u = t - 1
                    pool.wait_ge(L2["mv3"], u + 1)
                    nc.gpsimd.tensor_tensor(veps3[:, :], mv3[:, 1:2], ln_eps[:, :], ALU.add)\
                        .then_inc(L2["veps3"], 1)
                    pool.wait_ge(L2["veps3"], u + 1)
                    nc.gpsimd.tensor_tensor(rstd3[:, :], veps3[:, :], minus_half[:, 0:1], ALU.pow)\
                        .then_inc(L2["rstd3"], 1)
                if active(t, 0):
                    norm_scale(L2, t, s)
                    keep_rows(L2, t, s)

                if active(t, 1):
                    u = t - 1
                    pool.wait_ge(L2["xT"], u + 1)
                    nc.gpsimd.tensor_copy(XT[:, :, tile_cols(u)], xT_tile[:, 1 - s, :, :]).then_inc(L2["xT_all"], 1)

            over_tiles(pool, step2, lag=1)

            with pool.If(needed(pool)):
                with pool.Fori(0, TILES) as t:
                    pool.wait_ge(G["mv"], t + 1)
                    nc.gpsimd.tensor_tensor(veps3[:, :], mv3[:, 1:2], ln_eps[:, :], ALU.add).then_inc(G["veps"], 1)
                    pool.wait_ge(G["veps"], t + 1)
                    nc.gpsimd.tensor_tensor(rstd3[:, :], veps3[:, :], minus_half[:, 0:1], ALU.pow)\
                        .then_inc(G["rstd"], 1)

        @block.scalar
        def _(act):
            for dst, src in ((XT[:, :, :], xT), (w0_sb[:, :, :], w0)):
                act.dma_start(dst, src).then_inc(xT_in, 16)
            for s, src in ((0, hwvT), (1, hwo)):
                act.dma_start(stage[:, s, :], src).then_inc(stage_vo_in, 16)
            def row_sum(t, s):
                act.wait_ge(row_in[s], loaded(t, s))
                wait(act, row_summed, t)
                nc.scalar.activation(opB_hi[:, 0:8, :].rearrange("p a b -> p (a b)"), raw[:, s, :], ACT.Copy,
                                     accum_out=deg[:, bass.ds(t, 1)]).then_inc(row_summed, 1)

            over_tiles(act, row_sum)
            weights = ((X[:, :, :], x), (wqT_sb[:, :, :], wqT), (wkT_sb[:, :, :], wkT), (wvT_sb[:, :, :], wvT),
                       (bq_sb[:, :], bq), (bk_sb[:, :], bk), (bv_sb[:, :], bv), (ident[:, :], ident_in),
                       (diag[:, :], adj_diag))
            for dst, src in weights:
                act.dma_start(dst, src).then_inc(w_in, 16)
            act.wait_ge(row_summed, TILES)
            for c in range(DC):
                act.wait_ge(wvo_ps, 1)
                nc.scalar.activation(wvo_sb[:, c, :], wvo_out[c], ACT.Copy).then_inc(wvo_ready, 1)
            for s, src in ((0, hwq), (1, hwk)):
                act.dma_start(stage[:, s, :], src).then_inc(stage_qk_in, 16)
            act.wait_ge(consts, 5)
            for s in range(2):
                act.wait_ge(stage_qk_in, 32)
                wait(act, norms_done, s)
                nc.scalar.activation(opB_hi[:, 0:4, :].rearrange("p a b -> p (a b)"), stage[:, s, :], ACT.Square,
                                     accum_out=sums[:, 1 + s:2 + s]).then_inc(norms_done, 1)
            act.wait_ge(norms_done, 2)
            act.wait_ge(pow_done, 1)

            def operand_hi(t):
                act.wait_ge(xw_done, t // 2 * 2 + 2)
                nc.scalar.activation(opA_hi[:, t, :], xw_out(t), ACT.Copy, scale=dinv[:, t:t + 1])\
                    .then_inc(z_hi, 1)

            def split_hi(L, t, s, q):
                if q == 0:
                    act.wait_ge(L[f"in{s}"], loaded(t, s))
                wait(act, L["chunk_used"], (t - 1) * CHUNKS + q + 1)
                nc.scalar.activation(part_hi[:, q, :], raw[:, s, q * BLK:(q + 1) * BLK], ACT.Copy)\
                    .then_inc(L["hi"], 1)

            def step0(t, s):
                for q in range(CHUNKS):
                    if isinstance(t, int) and t == 0:
                        for j in range(q * SUB, (q + 1) * SUB):
                            operand_hi(j)
                    if active(t, 0):
                        split_hi(L0, t, s, q)
                    if isinstance(t, int) and t == 0 and q == 1:
                        act.wait_ge(w_in, 16 * len(weights))
                        nc.scalar.activation(ident_r[:, :], ident[:, :], ACT.Copy).then_inc(ident_ready, 1)
                    if q == 1 and active(t, 2):
                        v = t - 2
                        act.wait_ge(L0["xn"], v + 1)
                        nc.scalar.activation(opB_hi[:, v, :], xn[:, s, :], ACT.Copy).then_inc(L0["op_hi"], 1)

            over_tiles(act, step0, lag=2)

            def step1(t, s):
                for q in range(CHUNKS):
                    if active(t, 0):
                        split_hi(L1, t, s, q)
                    if q == 0 and active(t, 3):
                        w = t - 3
                        act.wait_ge(L1["xT_ps"], w + 1)
                        wait(act, L1["value_ps"], w - 1)
                        wait(act, L1["xT_all"], w - 1)
                        nc.scalar.activation(xT_tile[:, 1 - s, :, :], xT_out1, ACT.Copy).then_inc(L1["xT"], 1)
                    if q == 1 and active(t, 0):
                        wait(act, L1["signs"], t)
                        nc.scalar.activation(sign_out[:, :], raw[:, s, :], ACT.Sign, bias=below_one[:, :],
                                             accum_out=signs[:, bass.ds(t, 1)]).then_inc(L1["signs"], 1)
                    if q == 2 and active(t, 3):
                        w = t - 3
                        act.wait_ge(L1["key_ps"], w + 1)
                        for c in range(DC):
                            nc.scalar.activation(keyT_hi[:, c, tile_cols(w)], key_out[:, c, :], ACT.Identity,
                                                 bias=bk_sb[:, c:c + 1]).then_inc(L1["key_hi"], 1)
                        act.wait_ge(L1["value"], w + 1)
                        nc.scalar.activation(opA_hi[:, w, :], vf[:, :], ACT.Copy).then_inc(L1["value_hi"], 1)
                if active(t, 1):
                    u = t - 1
                    act.wait_ge(L1["chunk_used"], (u + 1) * CHUNKS)
                    wait(act, L1["sum"], u)
                    nc.scalar.activation(branch[:, :], acc_edges[1 - s], ACT.Copy,
                                         scale=rcount[:, bass.ds(u, 1)]).then_inc(L1["branch"], 1)

            over_tiles(act, step1, lag=3, peel=4)

            def weights_hi(u, q):
                act.wait_ge(L2["tr_ps"], u * CHUNKS + q + 1)
                wait(act, L2["attended"], (u - 1) * CHUNKS + q + 1)
                nc.scalar.activation(part_hi[:, q, :], bank[q % 2][:, :], ACT.Copy).then_inc(L2["w_hi"], 1)

            def step2(t, s):
                if active(t, 2):
                    weights_hi(t - 2, 0)
                    weights_hi(t - 2, 1)
                if active(t, 1):
                    u = t - 1
                    act.wait_ge(L2["nmax"], u + 1)
                    wait(act, L2["rsum"], u - 1)
                    nc.scalar.activation(raw[:, 1 - s, :], raw[:, 1 - s, :], ACT.Exp, bias=nmax[:, 1 - s, :],
                                         accum_out=wsum[:, 1 - s, :]).then_inc(L2["exp"], 1)
                if active(t, 0):
                    act.wait_ge(L2["qf"], DC * (t + 1))
                    wait(act, L2["scores"], t)
                    nc.scalar.activation(q_hi[:, :, :], qf[:, :, :], ACT.Copy).then_inc(L2["q_hi"], 1)
                if active(t, 2):
                    weights_hi(t - 2, 2)
                if active(t, 3):
                    u = t - 3
                    act.wait_ge(L2["xT_ps"], u + 1)
                    wait(act, L2["mixed"], u - 1)
                    wait(act, L2["xT_all"], u - 1)
                    act.wait_ge(L2["qf"], DC * (t + 1) if active(t, 0) else DC * TILES)
                    nc.scalar.activation(xT_tile[:, 1 - s, :, :], xT_out2, ACT.Copy).then_inc(L2["xT"], 1)
                if active(t, 2):
                    weights_hi(t - 2, 3)

            over_tiles(act, step2, lag=3, peel=4)

            with act.If(needed(act)):
                def head_operands(h):
                    act.wait_ge(G["key_ps"], h + 1)
                    nc.scalar.activation(head_key_hi, head_key_out, ACT.Copy).then_inc(G["key_hi"], 1)
                    act.wait_ge(G["value_ps"], h + 1)
                    for k in range(2):
                        nc.scalar.activation(head_value_hi[:, k * TILES // 2:(k + 1) * TILES // 2, :],
                                             head_value_out[k], ACT.Copy).then_inc(G["value_hi"], 1)

                def tile(n, t):
                    act.wait_ge(G["qf"], n + 1)
                    nc.scalar.activation(head_q_hi, head_qf, ACT.Copy).then_inc(G["q_hi"], 1)
                    act.wait_ge(G["mx"], 2 * n + 2)
                    nc.scalar.activation(scores_sb, scores_sb, ACT.Exp, bias=nmax[:, 0, :],
                                         accum_out=wsum[:, 0, :]).then_inc(G["exp"], 1)
                    for q in range(CHUNKS):
                        act.wait_ge(G["tr_ps"], n * CHUNKS + q + 1)
                        nc.scalar.activation(part_hi[:, q, :], bank[q % 2][:, :], ACT.Copy).then_inc(G["w_hi"], 1)
                    act.wait_ge(G["head_t_ps"], n + 1)
                    nc.scalar.activation(head_T, head_T_out, ACT.Copy).then_inc(G["head_t"], 1)

                heads_and_tiles(act, head_operands, tile)

        @block.vector
        def _(dve):
            def row_count(t, s):
                dve.wait_ge(row_in[s], loaded(t, s))
                wait(dve, row_counted, t)
                nc.vector.tensor_scalar(opB_lo[:, 0:8, :].rearrange("p a b -> p (a b)"), raw[:, s, :], 0.0, 0.0,
                                        ALU.is_gt, ALU.add, accum_out=count[:, bass.ds(t, 1)])\
                    .then_inc(row_counted, 1)

            over_tiles(dve, row_count)
            dve.wait_ge(row_summed, TILES)
            dve.wait_ge(row_counted, TILES)
            nc.vector.tensor_scalar(deg1[:, :], deg[:, :], 1.0, None, ALU.add).then_inc(degree_step, 1)
            nc.vector.tensor_scalar(count_safe[:, :], count[:, :], EDGE_EPS ** 2, None, ALU.max)\
                .then_inc(degree_step, 1)
            dve.wait_ge(pow_done, 2)
            nc.vector.tensor_tensor(head_sum[:, :], count[:, :], rcount[:, :], ALU.mult).then_inc(degree_step, 1)
            dve.wait_ge(degree_step, 3)
            nc.vector.tensor_tensor(edge_deg[:, :], head_sum[:, :], deg[:, :], ALU.add).then_inc(degree_step, 1)
            dve.wait_ge(degree_step, 4)
            nc.vector.reciprocal(redge[:, :], edge_deg[:, :]).then_inc(degree_step, 1)
            def operand_lo(t):
                dve.wait_ge(z_hi, t // 2 * 2 + 2)
                nc.vector.scalar_tensor_tensor(opA_lo[:, t, :], xw_out(t), dinv[:, t:t + 1], f32(opA_hi[:, t, :]),
                                               ALU.mult, ALU.subtract).then_inc(z_lo, 1)

            def split_lo(L, t, s, q):
                dve.wait_ge(L["hi"], t * CHUNKS + q + 1)
                nc.vector.tensor_tensor(part_lo[:, q, :], raw[:, s, q * BLK:(q + 1) * BLK], f32(part_hi[:, q, :]),
                                        ALU.subtract).then_inc(L["lo"], 1)

            def statistics(L, u, b):
                dve.wait_ge(L["y"], u + 1)
                nc.vector.bn_stats(stats[:, b, :], ysum[:, b, :]).then_inc(L["stats"], 1)
                dve.wait_ge(L["stats"], u + 1)
                wait(dve, L["rstd"], u - 1)
                own_instruction(dve, dve_held)
                nc.vector.bn_aggr(mv[:, b, :], stats[:, b, :]).then_inc(L["mv"], 1)

            def norm(L, u, b):
                dve.wait_ge(L["rstd"], u + 1)
                wait(dve, L["rows"], u - 1)
                nc.vector.tensor_scalar(xn[:, b, :], ysum[:, b, :], mv[:, b, 0:1], rstd[:, b, :],
                                        ALU.subtract, ALU.mult).then_inc(L["xn"], 1)

            def step0(t, s):
                for q in range(CHUNKS):
                    if isinstance(t, int) and t == 0:
                        for j in range(q * SUB, (q + 1) * SUB):
                            operand_lo(j)
                    if active(t, 0):
                        split_lo(L0, t, s, q)
                    if q == 1 and active(t, 2):
                        v = t - 2
                        wait(dve, L0["op_hi"], v - 1)
                        wait(dve, L0["op_lo"], v - 1)
                        norm(L0, v, s)
                        dve.wait_ge(L0["op_hi"], v + 1)
                        nc.vector.tensor_tensor(opB_lo[:, v, :], xn[:, s, :], f32(opB_hi[:, v, :]), ALU.subtract)\
                            .then_inc(L0["op_lo"], 1)
                if active(t, 1):
                    b, u = 1 - s, t - 1
                    if isinstance(t, int) and t == 1:
                        dve.wait_ge(w_in, 16 * 9)
                    dve.wait_ge(L0["acc"], u + 1)
                    wait(dve, L0["y"], u)
                    nc.vector.tensor_scalar(branch[:, :], acc_weighted[b], dinv[:, bass.ds(u, 1)], 0.0,
                                            ALU.mult, ALU.max).then_inc(L0["branch"], 1)
                    dve.wait_ge(L0["branch"], u + 1)
                    nc.vector.tensor_tensor(ysum[:, b, :], branch[:, :], X[:, u, :], ALU.add).then_inc(L0["y"], 1)
                    statistics(L0, u, b)

            over_tiles(dve, step0, lag=2, peel=4)

            def step1(t, s):
                for q in range(CHUNKS):
                    if active(t, 0):
                        split_lo(L1, t, s, q)
                        nc.vector.tensor_scalar(edges[:, q, :], raw[:, s, q * BLK:(q + 1) * BLK], 0.0, None,
                                                ALU.is_gt).then_inc(L1["edges"], 1)
                    if q == 0 and active(t, 2):
                        wait(dve, L1["xT_ps"], t - 3)
                        norm(L1, t - 2, s)
                    if q == 2 and active(t, 3):
                        w = t - 3
                        dve.wait_ge(L1["value_ps"], w + 1)
                        wait(dve, L1["value_hi"], w)
                        wait(dve, L1["value_lo"], w)
                        nc.vector.tensor_tensor(vf[:, :], value_out, bv_sb[:, :], ALU.add).then_inc(L1["value"], 1)
                        dve.wait_ge(L1["key_hi"], DC * w + DC)
                        for c in range(DC):
                            nc.vector.scalar_tensor_tensor(keyT_lo[:, c, tile_cols(w)], key_out[:, c, :],
                                                           bk_sb[:, c:c + 1], f32(keyT_hi[:, c, tile_cols(w)]),
                                                           ALU.add, ALU.subtract).then_inc(L1["key_lo"], 1)
                        dve.wait_ge(L1["value_hi"], w + 1)
                        nc.vector.tensor_tensor(opA_lo[:, w, :], vf[:, :], f32(opA_hi[:, w, :]), ALU.subtract)\
                            .then_inc(L1["value_lo"], 1)
                if active(t, 1):
                    b, u = 1 - s, t - 1
                    dve.wait_ge(L1["branch"], u + 1)
                    nc.vector.tensor_tensor(ysum[:, b, :], acc_weighted[b], branch[:, :], ALU.add)\
                        .then_inc(L1["sum"], 1)
                    dve.wait_ge(L1["sum"], u + 1)
                    nc.vector.scalar_tensor_tensor(ysum[:, b, :], ysum[:, b, :], redge[:, bass.ds(u, 1)],
                                                   X[:, u, :], ALU.mult, ALU.add).then_inc(L1["y"], 1)
                    statistics(L1, u, b)

            over_tiles(dve, step1, lag=3, peel=4)

            dve.wait_ge(L1["signs"], TILES)
            nc.vector.tensor_scalar(diag_sign[:, :], diag[:, :], 1.0 - 2.0 ** -24, None, ALU.is_gt)\
                .then_inc(flag_step, 1)
            nc.vector.tensor_scalar(diag_least[:, :], diag[:, :], 1.0 - 2.0 ** -24, None, ALU.is_ge)\
                .then_inc(flag_step, 1)
            dve.wait_ge(flag_step, 2)
            nc.vector.tensor_tensor(diag_sign[:, :], diag_sign[:, :], diag_least[:, :], ALU.add).then_inc(flag_step, 1)
            dve.wait_ge(flag_step, 3)
            nc.vector.tensor_tensor(signs[:, :], signs[:, :], diag_sign[:, :], ALU.subtract).then_inc(flag_step, 1)
            dve.wait_ge(flag_step, 4)
            nc.vector.tensor_scalar(signs[:, :], signs[:, :], float(N), None, ALU.add).then_inc(flag_step, 1)
            dve.wait_ge(flag_step, 5)
            nc.vector.reduce_sum(sums[:, 0:1], signs[:, :], axis=AX.X).then_inc(flag_step, 1)

            def needs_general_path():
                dve.wait_ge(totals_done, 1)
                nc.vector.tensor_copy(flag[0:1, 0:4], totals).then_inc(flag_step, 1)
                dve.wait_ge(flag_step, 7)
                nc.vector.tensor_tensor(flag[0:1, 4:5], flag[0:1, 1:2], flag[0:1, 2:3], ALU.mult)\
                    .then_inc(flag_step, 1)
                dve.wait_ge(flag_step, 8)
                nc.vector.tensor_scalar(flag[0:1, 5:6], flag[0:1, 4:5], NORMS_BOUND, None, ALU.is_ge)\
                    .then_inc(flag_step, 1)
                dve.wait_ge(flag_step, 9)
                nc.vector.tensor_tensor(flag_int[0:1, :], flag[0:1, 0:1], flag[0:1, 5:6], ALU.add)\
                    .then_inc(flag_step, 1)


            def weights_lo(u, q):
                dve.wait_ge(L2["w_hi"], u * CHUNKS + q + 1)
                nc.vector.tensor_tensor(part_lo[:, q, :], bank[q % 2][:, :], f32(part_hi[:, q, :]),
                                        ALU.subtract).then_inc(L2["w_lo"], 1)

            def step2(t, s):
                if isinstance(t, int) and t == 2:
                    needs_general_path()
                if active(t, 4):
                    u = t - 4
                    dve.wait_ge(L2["mixed"], u + 1)
                    nc.vector.tensor_tensor(y3[:, :], mixed, xn[:, s, :], ALU.add).then_inc(L2["y3"], 1)
                    dve.wait_ge(L2["y3"], u + 1)
                    nc.vector.bn_stats(stats3[:, :], y3[:, :]).then_inc(L2["stats3"], 1)
                    dve.wait_ge(L2["stats3"], u + 1)
                    own_instruction(dve, dve_held)
                    nc.vector.bn_aggr(mv3[:, :], stats3[:, :]).then_inc(L2["mv3"], 1)
                if active(t, 3):
                    b, u = 1 - s, t - 3
                    dve.wait_ge(L2["attended"], (u + 1) * CHUNKS)
                    dve.wait_ge(L2["exp"], u + 1)
                    nc.vector.reciprocal(rsum[:, :], wsum[:, b, :]).then_inc(L2["rsum"], 1)
                    dve.wait_ge(L2["rsum"], u + 1)
                    nc.vector.scalar_tensor_tensor(ysum[:, b, :], attended, rsum[:, :], X[:, u, :],
                                                   ALU.mult, ALU.add).then_inc(L2["y"], 1)
                    statistics(L2, u, b)
                if active(t, 4):
                    u = t - 4
                    dve.wait_ge(L2["rstd3"], u + 1)
                    wait(dve, L2[f"stored{s}"], (u - s) * 8)
                    nc.vector.tensor_scalar(out_tile[:, s, :], y3[:, :], mv3[:, 0:1], rstd3[:, :],
                                            ALU.subtract, ALU.mult).then_inc(L2["out"], 1)
                if active(t, 1):
                    b, u = 1 - s, t - 1
                    dve.wait_ge(L2[f"in{b}"], loaded(u, b))
                    wait(dve, L2["mx"], u)
                    for q in range(CHUNKS):
                        dve.wait_ge(L2["scores"], (u * CHUNKS) + q + 1)
                        own_instruction(dve, dve_held)
                        part = raw[:, b, q * BLK:(q + 1) * BLK]
                        nc.vector.tensor_tensor_reduce(out=part, in0=wide[:, q, :], in1=part, scale=2.0,
                                                       scalar=LOWEST, op0=ALU.add, op1=ALU.max,
                                                       accum_out=mx[:, q:q + 1]).then_inc(L2["masked"], 1)
                        if q == 1 and active(t, 3):
                            norm(L2, t - 3, b)
                    dve.wait_ge(L2["masked"], (u + 1) * CHUNKS)
                    wait(dve, L2["exp"], u - 1)
                    nc.vector.reduce_max(nmax[:, b, :], mx[:, :], axis=AX.X).then_inc(L2["mx"], 1)
                    dve.wait_ge(L2["mx"], u + 1)
                    nc.vector.tensor_scalar(nmax[:, b, :], nmax[:, b, :], -1.0, None, ALU.mult)\
                        .then_inc(L2["nmax"], 1)
                elif active(t, 3):
                    norm(L2, t - 3, 1 - s)
                if active(t, 2):
                    weights_lo(t - 2, 0)
                    weights_lo(t - 2, 1)
                if active(t, 0):
                    dve.wait_ge(L2["q_ps"], t + 1)
                    wait(dve, L2["q_hi"], t)
                    wait(dve, L2["q_lo"], t)
                    for c in range(DC):
                        nc.vector.tensor_scalar(qf[:, c, :], q_out[:, c, :], bq_sb[:, c:c + 1], ATT_SCALE / 2,
                                                ALU.add, ALU.mult).then_inc(L2["qf"], 1)
                    dve.wait_ge(L2["q_hi"], t + 1)
                    nc.vector.tensor_tensor(q_lo[:, :, :], qf[:, :, :], f32(q_hi[:, :, :]), ALU.subtract)\
                        .then_inc(L2["q_lo"], 1)
                if active(t, 2):
                    weights_lo(t - 2, 2)
                    weights_lo(t - 2, 3)

            over_tiles(dve, step2, lag=4, peel=4)

            with dve.If(needed(dve)):
                dve.wait_ge(L2["out"], TILES)
                dve.wait_ge(L2["xT_all"], TILES)
                dve.wait_ge(L2["stored0"], 16 * TILES // 2)
                dve.wait_ge(L2["stored1"], 16 * TILES // 2)
                nc.vector.memset(head_padded[:, :], 0.0).then_inc(G["zeroed"], 1)
                dve.wait_ge(G["zeroed"], 1)
                nc.vector.memset(mx[:, :], 0.0).then_inc(G["taken"], 1)
                dve.wait_ge(G["taken"], 1)
                nc.vector.memset(mx[:, :], 0.0).then_inc(G["added"], 1)

                def head_operands(h):
                    dve.wait_ge(G["key_hi"], h + 1)
                    nc.vector.tensor_tensor(head_key_lo, head_key_out.rearrange("p q n -> p (q n)"), f32(head_key_hi),
                                            ALU.subtract).then_inc(G["key_lo"], 1)
                    dve.wait_ge(G["value_hi"], h * 2 + 2)
                    for k in range(2):
                        part = slice(k * TILES // 2, (k + 1) * TILES // 2)
                        nc.vector.tensor_tensor(head_value_lo[:, part, :], head_value_out[k],
                                                f32(head_value_hi[:, part, :]), ALU.subtract)\
                            .then_inc(G["value_lo"], 1)

                def tile(n, t):
                    dve.wait_ge(G["q_ps"], n + 1)
                    nc.vector.tensor_scalar(head_qf, head_q_out, HEAD_SCALE, None, ALU.mult).then_inc(G["qf"], 1)
                    dve.wait_ge(G["q_hi"], n + 1)
                    nc.vector.tensor_tensor(head_q_lo, head_qf, f32(head_q_hi), ALU.subtract).then_inc(G["q_lo"], 1)
                    dve.wait_ge(G["adj_in"], n * 16 + 16)
                    on_diagonal = adj_sb[:, tile_cols(t)]
                    nc.vector.tensor_tensor(on_diagonal, on_diagonal, ident[:, :], ALU.max).then_inc(G["penalty"], 1)
                    dve.wait_ge(G["penalty"], 2 * n + 1)
                    nc.vector.tensor_scalar(adj_sb, adj_sb, -1.0, 1.0, ALU.mult, ALU.add).then_inc(G["penalty"], 1)
                    dve.wait_ge(G["scores"], n + 1)
                    dve.wait_ge(G["penalty"], 2 * n + 2)
                    nc.vector.scalar_tensor_tensor(scores_sb, adj_sb, -MASK_VAL, wide[:, :, :].rearrange("p q n -> p (q n)"),
                                                   ALU.mult, ALU.add).then_inc(G["taken"], 1)
                    dve.wait_ge(G["taken"], n + 2)
                    on_diagonal = scores_sb[:, tile_cols(t)]
                    nc.vector.scalar_tensor_tensor(on_diagonal, ident[:, :], IDENTITY_BIAS, on_diagonal,
                                                   ALU.mult, ALU.add).then_inc(G["masked"], 1)
                    dve.wait_ge(G["masked"], n + 1)
                    nc.vector.reduce_max(nmax[:, 1, :], scores_sb, axis=AX.X).then_inc(G["mx"], 1)
                    dve.wait_ge(G["mx"], 2 * n + 1)
                    nc.vector.tensor_scalar(nmax[:, 0, :], nmax[:, 1, :], -1.0, None, ALU.mult).then_inc(G["mx"], 1)
                    for q in range(CHUNKS):
                        dve.wait_ge(G["w_hi"], n * CHUNKS + q + 1)
                        nc.vector.tensor_tensor(part_lo[:, q, :], bank[q % 2][:, :], f32(part_hi[:, q, :]),
                                                ALU.subtract).then_inc(G["w_lo"], 1)
                    dve.wait_ge(G["exp"], n + 1)
                    nc.vector.reciprocal(rsum[:, :], wsum[:, 0, :]).then_inc(G["rsum"], 1)
                    dve.wait_ge(G["attended"], n + 1)
                    dve.wait_ge(G["rsum"], n + 1)
                    nc.vector.tensor_scalar(head_padded[:, 0:KD], head_attended, rsum[:, :], None, ALU.mult)\
                        .then_inc(G["head"], 1)
                    dve.wait_ge(G["mixed"], n + 1)
                    nc.vector.tensor_tensor(X[:, t, :], X[:, t, :], head_mixed, ALU.add).then_inc(G["added"], 1)

                heads_and_tiles(dve, head_operands, tile)
                dve.wait_ge(G["added"], HEADS * TILES + 1)
                for s in range(2):
                    dve.sem_inc(G[f"stored{s}"], 16)
                with dve.Fori(0, TILES // 2) as pair:
                    for s in range(2):
                        t = pair * 2 + s
                        nc.vector.bn_stats(stats3[:, :], X[:, t, :]).then_inc(G["stats"], 1)
                        dve.wait_ge(G["stats"], t + 1)
                        own_instruction(dve, dve_held)
                        nc.vector.bn_aggr(mv3[:, :], stats3[:, :]).then_inc(G["mv"], 1)
                        dve.wait_ge(G["rstd"], t + 1)
                        dve.wait_ge(G[f"stored{s}"], pair * 16 + 16)
                        nc.vector.tensor_scalar(out_tile[:, s, :], X[:, t, :], mv3[:, 0:1], rstd3[:, :],
                                                ALU.subtract, ALU.mult).then_inc(G["normed"], 1)

        @block.tensor
        def _(pe):
            pe.wait_ge(stage_vo_in, 32)
            for c in range(DC):
                for k in range(HK // P):
                    last = nc.tensor.matmul(wvo_out[c], stage[:, 0, k * D + c * P:k * D + (c + 1) * P],
                                            stage[:, 1, k * D:(k + 1) * D], start=k == 0, stop=k == HK // P - 1)
            last.then_inc(wvo_ps, 1)
            pe.wait_ge(xT_in, 32)
            for t in range(TILES):
                if t == TILES - 2:
                    pe.wait_ge(wvo_ready, DC)
                for c in range(DC):
                    last = nc.tensor.matmul(xw_out(t), XT[:, c, t * P:(t + 1) * P], w0_sb[:, c, :],
                                            start=c == 0, stop=c == DC - 1)
                last.then_inc(xw_done, 1)

            def weighted_sum(L, t, s, q, op_hi, op_lo, last_tile_stop):
                pe.wait_ge(L["lo"], t * CHUNKS + q + 1)
                if L is L1:
                    pe.wait_ge(L1["edges"], t * CHUNKS + q + 1)
                for k in range(SUB):
                    j = q * SUB + k
                    hi, lo, edge = (part[:, q, k * P:(k + 1) * P] for part in (part_hi, part_lo, edges))
                    first, end = j == 0, j == TILES - 1
                    nc.tensor.matmul(acc_weighted[s], hi, op_hi[:, j, :], start=first, stop=False)
                    nc.tensor.matmul(acc_weighted[s], hi, op_lo[:, j, :], start=False, stop=False)
                    last = nc.tensor.matmul(acc_weighted[s], lo, op_hi[:, j, :], start=False,
                                            stop=end and last_tile_stop)
                    if L is L1:
                        nc.tensor.matmul(acc_edges[s], edge, op_hi[:, j, :], start=first, stop=False)
                        last = nc.tensor.matmul(acc_edges[s], edge, op_lo[:, j, :], start=False, stop=end)
                last.then_inc(L["chunk_used"], 1)

            def step0(t, s):
                wait(pe, L0["branch"], t - 1)
                for q in range(CHUNKS):
                    if isinstance(t, int) and t == 0:
                        pe.wait_ge(z_lo, (q + 1) * SUB)
                    weighted_sum(L0, t, s, q, opA_hi, opA_lo, False)
                if isinstance(t, int) and t == 0:
                    pe.wait_ge(ident_ready, 1)
                nc.tensor.matmul(acc_weighted[s], ident_r[:, :], opA_hi[:, t, :], start=False, stop=False)
                nc.tensor.matmul(acc_weighted[s], ident_r[:, :], opA_lo[:, t, :], start=False, stop=True)\
                    .then_inc(L0["acc"], 1)

            over_tiles(pe, step0)

            pe.wait_ge(L0["op_lo"], TILES)
            pe.wait_ge(L0["branch"], TILES)

            def step1(t, s):
                for q in range(CHUNKS):
                    if active(t, 0):
                        if q == 0:
                            wait(pe, L1["sum"], t - 1)
                        weighted_sum(L1, t, s, q, opB_hi, opB_lo, True)
                    if q == 0 and active(t, 2):
                        v = t - 2
                        pe.wait_ge(L1["xn"], v + 1)
                        wait(pe, L1["xT"], v)
                        for c in range(DC):
                            last = nc.tensor.transpose(xT_out1[:, c, :], xn[:, s, c * P:(c + 1) * P], ident[:, :])
                        last.then_inc(L1["xT_ps"], 1)
                    if q == 2 and active(t, 2):
                        v = t - 2
                        pe.wait_ge(L1["xT"], v + 1)
                        wait(pe, L1["key_lo"], DC * v)
                        wait(pe, L1["value"], v)
                        for o in range(DC):
                            for c in range(DC):
                                last = nc.tensor.matmul(key_out[:, o, :], wkT_sb[:, c, o * P:(o + 1) * P],
                                                        xT_tile[:, s, c, :], start=c == 0, stop=c == DC - 1)
                        last.then_inc(L1["key_ps"], 1)
                        for c in range(DC):
                            last = nc.tensor.matmul(value_out, xT_tile[:, s, c, :], wvT_sb[:, c, :],
                                                    start=c == 0, stop=c == DC - 1)
                        last.then_inc(L1["value_ps"], 1)

            over_tiles(pe, step1, lag=2)
            pe.wait_ge(L1["key_lo"], DC * TILES)
            pe.wait_ge(L1["value_lo"], TILES)
            pe.wait_ge(L1["xT_all"], TILES)

            def step2(t, s):
                if isinstance(t, int) and t == 2:
                    pe.wait_ge(flag_step, 6)
                    pe.wait_ge(norms_done, 2)
                    nc.tensor.matmul(totals, ones[:, 0:1], sums[:, :], start=True, stop=True)\
                        .then_inc(totals_done, 1)
                if active(t, 1):
                    u = t - 1
                    pe.wait_ge(L2["q_lo"], u + 1)
                    for q in range(CHUNKS):
                        wait(pe, L2["masked"], (u - 1) * CHUNKS + q + 1)
                        for c in range(DC):
                            keys = slice(q * BLK, (q + 1) * BLK)
                            nc.tensor.matmul(wide[:, q, :], q_hi[:, c, :], keyT_hi[:, c, keys], start=c == 0, stop=False)
                            nc.tensor.matmul(wide[:, q, :], q_hi[:, c, :], keyT_lo[:, c, keys], start=False, stop=False)
                            last = nc.tensor.matmul(wide[:, q, :], q_lo[:, c, :], keyT_hi[:, c, keys],
                                                    start=False, stop=c == DC - 1)
                        last.then_inc(L2["scores"], 1)
                v = t - 2

                def transpose_weights(q):
                    if q == 0:
                        pe.wait_ge(L2["exp"], v + 1)
                    wait(pe, L2["w_lo"], v * CHUNKS + q - 1)
                    for k in range(SUB):
                        j = q * SUB + k
                        last = nc.tensor.transpose(bank[q % 2][:, k * P:(k + 1) * P],
                                                   raw[:, s, j * P:(j + 1) * P], ident[:, :])
                    last.then_inc(L2["tr_ps"], 1)

                def attend(q):
                    if isinstance(t, int) and t == 2 and q == 0:
                        pe.wait_ge(flag_step, 7)
                    if q == 0:
                        wait(pe, L2["y"], v)
                        wait(pe, L2["y3"], v - 1)
                    pe.wait_ge(L2["w_lo"], v * CHUNKS + q + 1)
                    for k in range(SUB):
                        j = q * SUB + k
                        hi, lo = (part[:, q, k * P:(k + 1) * P] for part in (part_hi, part_lo))
                        nc.tensor.matmul(attended, hi, opA_hi[:, j, :], start=j == 0, stop=False)
                        nc.tensor.matmul(attended, hi, opA_lo[:, j, :], start=False, stop=False)
                        last = nc.tensor.matmul(attended, lo, opA_hi[:, j, :], start=False, stop=j == TILES - 1)
                    last.then_inc(L2["attended"], 1)

                if active(t, 2):
                    transpose_weights(0)
                    transpose_weights(1)
                if active(t, 3):
                    u = t - 3
                    pe.wait_ge(L2["xn"], u + 1)
                    wait(pe, L2["xT"], u)
                    pe.wait_ge(L2["qf"], DC * t if active(t, 0) else DC * TILES)
                    for c in range(DC):
                        last = nc.tensor.transpose(xT_out2[:, c, :], xn[:, 1 - s, c * P:(c + 1) * P], ident[:, :])
                    last.then_inc(L2["xT_ps"], 1)
                if active(t, 0):
                    wait(pe, L2["qf"], DC * t)
                    if active(t, 4):
                        pe.wait_ge(L2["xT"], t - 3)
                    for o in range(DC):
                        for c in range(DC):
                            last = nc.tensor.matmul(q_out[:, o, :], wqT_sb[:, c, o * P:(o + 1) * P],
                                                    XT[:, c, tile_cols(t)], start=c == 0, stop=c == DC - 1)
                    last.then_inc(L2["q_ps"], 1)
                if active(t, 2):
                    attend(0)
                    transpose_weights(2)
                    attend(1)
                    transpose_weights(3)
                    attend(2)
                    attend(3)
                if active(t, 3):
                    u = t - 3
                    pe.wait_ge(L2["xT"], u + 1)
                    wait(pe, L2["y3"], u)
                    pe.wait_ge(L2["y"], u + 1)
                    for c in range(DC):
                        last = nc.tensor.matmul(mixed, xT_tile[:, 1 - s, c, :], wvo_sb[:, c, :],
                                                start=c == 0, stop=c == DC - 1)
                    last.then_inc(L2["mixed"], 1)

            over_tiles(pe, step2, lag=3, peel=4)

            with pe.If(needed(pe)):
                def head_operands(h):
                    pe.wait_ge(G["added"], h * TILES + 1)
                    pe.wait_ge(G["weights"], h * 64 + 64)
                    for q in range(CHUNKS):
                        for c in range(DC):
                            last = nc.tensor.matmul(head_key_out[:, q, :], head_wk[:, c, :],
                                                    XT[:, c, q * BLK:(q + 1) * BLK], start=c == 0, stop=c == DC - 1)
                    last.then_inc(G["key_ps"], 1)
                    for j in range(TILES):
                        for c in range(DC):
                            last = nc.tensor.matmul(head_value_out[j // 8][:, j % 8, :], XT[:, c, j * P:(j + 1) * P],
                                                    head_wv[:, c, :], start=c == 0, stop=c == DC - 1)
                    last.then_inc(G["value_ps"], 1)
                    pe.wait_ge(G["key_lo"], h + 1)
                    pe.wait_ge(G["value_lo"], h * 2 + 2)
                    own_instruction(pe, pe_held)

                def tile(n, t):
                    pe.wait_ge(G["added"], n + 1)
                    for c in range(DC):
                        last = nc.tensor.matmul(head_q_out, head_wq[:, c, :], XT[:, c, tile_cols(t)],
                                                start=c == 0, stop=c == DC - 1)
                    last.then_inc(G["q_ps"], 1)
                    pe.wait_ge(G["q_lo"], n + 1)
                    for q in range(CHUNKS):
                        keys = slice(q * BLK, (q + 1) * BLK)
                        nc.tensor.matmul(wide[:, q, :], head_q_hi, head_key_hi[:, keys], start=True, stop=False)
                        nc.tensor.matmul(wide[:, q, :], head_q_hi, head_key_lo[:, keys], start=False, stop=False)
                        last = nc.tensor.matmul(wide[:, q, :], head_q_lo, head_key_hi[:, keys], start=False, stop=True)
                    last.then_inc(G["scores"], 1)
                    pe.wait_ge(G["exp"], n + 1)
                    for q in range(CHUNKS):
                        if q >= 2:
                            pe.wait_ge(G["w_lo"], n * CHUNKS + q - 1)
                        for k in range(SUB):
                            j = q * SUB + k
                            last = nc.tensor.transpose(bank[q % 2][:, k * P:(k + 1) * P],
                                                       scores_sb[:, j * P:(j + 1) * P], ident[:, :])
                        last.then_inc(G["tr_ps"], 1)
                    for q in range(CHUNKS):
                        pe.wait_ge(G["w_lo"], n * CHUNKS + q + 1)
                        for k in range(SUB):
                            j = q * SUB + k
                            hi, lo = (part[:, q, k * P:(k + 1) * P] for part in (part_hi, part_lo))
                            nc.tensor.matmul(head_attended, hi, head_value_hi[:, j, :], start=j == 0, stop=False)
                            nc.tensor.matmul(head_attended, hi, head_value_lo[:, j, :], start=False, stop=False)
                            last = nc.tensor.matmul(head_attended, lo, head_value_hi[:, j, :], start=False,
                                                    stop=j == TILES - 1)
                    last.then_inc(G["attended"], 1)
                    pe.wait_ge(G["head"], n + 1)
                    nc.tensor.transpose(head_T_out, head_padded, ident[:, :]).then_inc(G["head_t_ps"], 1)
                    pe.wait_ge(G["head_t"], n + 1)
                    nc.tensor.matmul(head_mixed, head_T[0:KD, :], head_wo, start=True, stop=True)\
                        .then_inc(G["mixed"], 1)

                heads_and_tiles(pe, head_operands, tile)


def kernel(x, adj, L0_gnn_weight, L2_gnn_Wq, L2_gnn_bq, L2_gnn_Wk, L2_gnn_bk, L2_gnn_Wv, L2_gnn_bv,
           L3_gnn_Wks, L3_gnn_Wqs, L3_gnn_Wvs, L3_gnn_Wo):
    import numpy as np
    import concourse.bacc as bacc
    from concourse.bass_utils import run_bass_kernel_spmd

    x, adj = np.asarray(x), np.asarray(adj)

    def chunked(w):
        w = np.asarray(w)
        return w.reshape(-1, P, w.shape[1]).transpose(1, 0, 2)

    def heads_side_by_side(w):
        return np.asarray(w).transpose(1, 0, 2).reshape(D, HK)

    arrays = dict(
        x=x.reshape(TILES, P, D).transpose(1, 0, 2),
        xT=chunked(x.T),
        adj=adj,
        adjT=adj.reshape(TILES, P, TILES, P).transpose(0, 3, 2, 1).reshape(N, N),
        adj_diag=np.diagonal(adj).reshape(TILES, P).T,
        w0=chunked(L0_gnn_weight),
        wqT=chunked(np.asarray(L2_gnn_Wq).T), bq=np.asarray(L2_gnn_bq).reshape(DC, P).T,
        wkT=chunked(np.asarray(L2_gnn_Wk).T), bk=np.asarray(L2_gnn_bk).reshape(DC, P).T,
        wvT=chunked(np.asarray(L2_gnn_Wv).T), bv=np.broadcast_to(np.asarray(L2_gnn_bv), (P, D)),
        hwk=chunked(heads_side_by_side(L3_gnn_Wks)).reshape(P, -1),
        hwq=chunked(heads_side_by_side(L3_gnn_Wqs)).reshape(P, -1),
        hwv=chunked(heads_side_by_side(L3_gnn_Wvs)).reshape(P, -1),
        hwvT=chunked(heads_side_by_side(L3_gnn_Wvs).T).reshape(P, -1),
        hwo=chunked(np.asarray(L3_gnn_Wo).reshape(HK, D)).reshape(P, -1),
        hwo_rows=np.asarray(L3_gnn_Wo).reshape(HK, D),
        ident_in=np.eye(P, dtype=np.float32),
    )
    nc = bacc.Bacc("TRN2", target_bir_lowering=False, num_devices=1)
    arrays = {name: np.ascontiguousarray(a) for name, a in arrays.items()}
    args = {name: nc.dram_tensor(f"{name}_dram", a.shape, mybir.dt.from_np(a.dtype), kind="ExternalInput").ap()
            for name, a in arrays.items()}
    out = nc.dram_tensor("out_dram", (N, D), F32, kind="ExternalOutput").ap()
    build(nc, out=out, **args)
    r = run_bass_kernel_spmd(nc, [{f"{name}_dram": a for name, a in arrays.items()}], core_ids=[0])
    return r.results[0]["out_dram"]
```

```python
import concourse.bass as bass
from concourse import mybir
from contextlib import ExitStack

F32 = mybir.dt.float32
F32R = mybir.dt.float32r
I32 = mybir.dt.int32
ALU = mybir.AluOpType
ACT = mybir.ActivationFunctionType
AX = mybir.AxisListType

P = 128
N = 2048
D = 256
TILES = N // P
DC = D // P
BLK = 512
CHUNKS = N // BLK
SUB = BLK // P
HELD = 4
HEADS = 8
KD = 64
HK = HEADS * KD
LN_EPS = 1e-5
EDGE_EPS = 1e-12
ATT_SCALE = float(D) ** -0.5
HEAD_SCALE = float(KD) ** -0.5
IDENTITY_BIAS = 0.01
MASK_VAL = 1e16
LOWEST = -3.0e38
Z_LAG = 3
FLAG_STEPS = 10
NORMS_BOUND = (1e8 / (D * HEAD_SCALE)) ** 2


def active(t, lag, count=TILES):
    return not isinstance(t, int) or lag <= t < count + lag


def wait(eng, sem, value):
    if not isinstance(value, int) or value > 0:
        eng.wait_ge(sem, value)


def own_instruction(eng, held):
    eng.sem_inc(held, 1)


def over_tiles(eng, step, lag=0, count=TILES, peel=2, slots=2):
    for t in range(peel):
        step(t, t % slots)
    with eng.Fori(peel // slots, count // slots) as group:
        for s in range(slots):
            step(group * slots + s, s)
    for t in range(count, count + lag):
        step(t, t % slots)


def loaded(t, s, slots=2):
    return (t - s) * (16 // slots) + 16


def tile_cols(t):
    return bass.ds(t * P, P)


def f32(ap):
    return ap.bitcast(F32)


def build(nc, x, xT, adj, adjT, adj_diag, w0, wqT, bq, wkT, bk, wvT, bv, hwk, hwq, hwv, hwvT, hwo, hwo_rows,
          ident_in, out):
    with ExitStack() as ctx:
        def sb(name, shape, dt=F32):
            return ctx.enter_context(nc.sbuf_tensor(name, shape, dt))

        def sem(name):
            return ctx.enter_context(nc.semaphore(name))

        X = sb("X", [P, TILES, D])
        XT = sb("XT", [P, DC, N])
        opA_hi = sb("opA_hi", [P, TILES, D], F32R)
        opA_lo = sb("opA_lo", [P, TILES, D], F32R)
        opB_hi = sb("opB_hi", [P, TILES, D], F32R)
        opB_lo = sb("opB_lo", [P, TILES, D], F32R)
        keyT_hi = sb("keyT_hi", [P, DC, N], F32R)
        keyT_lo = sb("keyT_lo", [P, DC, N], F32R)
        raw = sb("raw", [P, 2, N])
        part_hi = sb("part_hi", [P, CHUNKS, BLK], F32R)
        part_lo = sb("part_lo", [P, CHUNKS, BLK], F32R)
        edges = sb("edges", [P, CHUNKS, BLK], F32R)
        w0_sb = sb("w0_sb", [P, DC, D])
        wqT_sb = sb("wqT_sb", [P, DC, D])
        wkT_sb = sb("wkT_sb", [P, DC, D])
        wvT_sb = sb("wvT_sb", [P, DC, D])
        bq_sb = sb("bq_sb", [P, DC])
        bk_sb = sb("bk_sb", [P, DC])
        bv_sb = sb("bv_sb", [P, D])
        stage = sb("stage", [P, 2, HK * D // P])
        wvo_sb = sb("wvo_sb", [P, DC, D])
        ident = sb("ident", [P, P])
        ident_r = sb("ident_r", [P, P], F32R)
        ones = sb("ones", [P, P])
        ones_r = sb("ones_r", [P, 1], F32R)
        deg_count = sb("deg_count", [P, 2, TILES])
        deg, count = deg_count[:, 0, :], deg_count[:, 1, :]
        sign_out = sb("sign_out", [P, N], mybir.dt.bfloat16)
        signs = sb("signs", [P, TILES])
        below_one = sb("below_one", [P, 1])
        diag = sb("diag", [P, TILES])
        diag_sign = sb("diag_sign", [P, TILES])
        diag_least = sb("diag_least", [P, TILES])
        deg1 = sb("deg1", [P, TILES])
        count_safe = sb("count_safe", [P, TILES])
        head_sum = sb("head_sum", [P, TILES])
        edge_deg = sb("edge_deg", [P, TILES])
        dinv = sb("dinv", [P, TILES])
        rcount = sb("rcount", [P, TILES])
        redge = sb("redge", [P, TILES])
        minus_half = sb("minus_half", [P, TILES])
        ln_eps = sb("ln_eps", [P, 1])
        sums = sb("sums", [P, 4])
        flag = sb("flag", [1, 8])
        flag_int = sb("flag_int", [1, 1], I32)
        branch = sb("branch", [P, D])
        ysum = sb("ysum", [P, 2, D])
        xn = sb("xn", [P, 2, D])
        stats = sb("stats", [P, 2, 6])
        mv = sb("mv", [P, 2, 2])
        veps = sb("veps", [P, 2, 1])
        rstd = sb("rstd", [P, 2, 1])
        xT_tile = sb("xT_tile", [P, 2, DC, P])
        vf = sb("vf", [P, D])
        qf = sb("qf", [P, DC, P])
        q_hi = sb("q_hi", [P, DC, P], F32R)
        q_lo = sb("q_lo", [P, DC, P], F32R)
        mx = sb("mx", [P, CHUNKS])
        nmax = sb("nmax", [P, 2, 1])
        wsum = sb("wsum", [P, 2, 1])
        rsum = sb("rsum", [P, 1])
        y3 = vf
        stats3 = sb("stats3", [P, 6])
        mv3 = sb("mv3", [P, 2])
        veps3 = sb("veps3", [P, 1])
        rstd3 = sb("rstd3", [P, 1])
        out_tile = sb("out_tile", [P, 2, D])

        psum = ctx.enter_context(nc.psum_tensor("psum", [P, 8, BLK], F32))
        wide = psum[:, 0:CHUNKS, :]
        bank = [psum[:, CHUNKS + i, :] for i in range(4)]

        row_slot = [raw[:, 0, :], raw[:, 1, :]] + [
            X[:, k * TILES // 2:(k + 1) * TILES // 2, :].rearrange("p t d -> p (t d)") for k in range(2)]
        held_hi, held_lo = ([half for buf in bufs for half in (buf[:, 0:N], buf[:, N:2 * N])] for bufs in (
            (keyT_hi[:, :, :].rearrange("p c n -> p (c n)"), opB_hi[:, :, :].rearrange("p t d -> p (t d)")),
            (keyT_lo[:, :, :].rearrange("p c n -> p (c n)"), opB_lo[:, :, :].rearrange("p t d -> p (t d)"))))
        held_acc = [wide[:, r, 0:D] for r in range(HELD)]
        held_rows_out = psum[0:1, CHUNKS:CHUNKS + 2, :]
        held_rows = xn[0:1, 0, :].rearrange("p (w i) -> p w i", w=2)
        held_columns = bank[0][:, 0:2]
        edges_flat = edges[:, :, :].rearrange("p q n -> p (q n)")
        xw_out = [bank[(v + 2) % 4][:, 0:D] for v in range(4)]
        wvo_out = [bank[3][:, c * D:(c + 1) * D] for c in range(DC)]
        totals = bank[2][0:1, 0:4]
        acc_weighted = [wide[:, s, 0:D] for s in range(2)]
        acc_edges = [wide[:, 2 + s, 0:D] for s in range(2)]
        xT_out1 = bank[0][:, 0:D].rearrange("p (c q) -> p c q", c=DC)
        key_out = bank[1][:, 0:D].rearrange("p (c q) -> p c q", c=DC)
        value_out = bank[2][:, 0:D]
        q_out = bank[3][:, 0:D].rearrange("p (c q) -> p c q", c=DC)
        xT_out2 = bank[3][:, D:2 * D].rearrange("p (c q) -> p c q", c=DC)
        attended = bank[2][:, 0:D]
        mixed = bank[2][:, D:2 * D]
        mixed_last = wide[:, 0, 0:D]

        def mixed_of(u):
            return mixed_last if isinstance(u, int) and u >= TILES - 3 else mixed

        ident_in_sem, x_in = sem("ident_in"), [sem(f"x_in{k}") for k in range(2)]
        xT_in, w_in, stage_vo_in, stage_qk_in = (sem(n) for n in ("xT_in", "w_in", "stage_vo_in", "stage_qk_in"))
        row_in = [sem(f"row_in{s}") for s in range(4)]
        row_summed, row_counted = sem("row_summed"), sem("row_counted")
        held_lo_done, held_summed, held_row, held_column, held_taken = (
            sem(n) for n in ("held_lo", "held_summed", "held_row", "held_column", "held_taken"))
        dve_held, pe_held = sem("dve_held"), sem("pe_held")
        consts, ones_ready, ident_ready = sem("consts"), sem("ones_ready"), sem("ident_ready")
        xw_done, wvo_ps, wvo_ready = sem("xw_done"), sem("wvo_ps"), sem("wvo_ready")
        norms_done, degree_step, flag_step = sem("norms_done"), sem("degree_step"), sem("flag_step")
        deg1_done, dinv_done, rcount_done = sem("deg1_done"), sem("dinv_done"), sem("rcount_done")
        z_hi, z_lo, totals_done = sem("z_hi"), sem("z_lo"), sem("totals_done")

        def named(prefix, names):
            return {n: sem(f"{prefix}_{n}") for n in names.split()}

        L0 = named("l0", "in0 in1 hi lo chunk_used acc branch y stats mv veps rstd xn rows op_hi op_lo")
        L1 = named("l1", "in0 in1 hi lo edges chunk_used branch sum y stats mv veps rstd xn rows "
                         "signs xT_ps xT xT_all key_ps key_hi key_lo value_ps value value_hi value_lo")
        L2 = named("l2", "in0 in1 q_ps qf q_hi q_lo scores masked mx nmax exp tr_ps w_hi w_lo attended "
                         "rsum y stats mv veps rstd xn rows xT_ps xT xT_all mixed "
                         "y3 stats3 mv3 veps3 rstd3 out stored0 stored1")

        G = named("l3", "weights key_ps key_hi key_lo value_ps value_hi value_lo adj_in q_ps qf q_hi q_lo "
                        "scores penalty taken masked mx exp tr_ps w_hi w_lo attended rsum head head_t_ps head_t mixed "
                        "added stats mv veps rstd normed stored0 stored1 zeroed")

        head_wq, head_wk, head_wv = (stage[:, 0, k * DC * KD:(k + 1) * DC * KD].rearrange("p (c k) -> p c k", c=DC)
                                     for k in range(3))
        head_wo = stage[0:KD, 1, 0:D]
        head_key_hi, head_key_lo = keyT_hi[0:KD, 0, :], keyT_lo[0:KD, 0, :]
        head_value_hi, head_value_lo = opA_hi[:, :, 0:KD], opA_lo[:, :, 0:KD]
        head_qf, head_q_hi, head_q_lo = qf[0:KD, 0, :], q_hi[0:KD, 0, :], q_lo[0:KD, 0, :]
        head_key_out = wide[0:KD, :, :]
        head_value_out = [bank[2 + k][:, :].rearrange("p (t k) -> p t k", t=TILES // 2) for k in range(2)]
        head_q_out = bank[3][0:KD, 0:P]
        head_attended = bank[2][:, 0:KD]
        head_padded = vf[:, 0:P]
        head_T_out, head_T = bank[3][:, 0:P], qf[:, 1, :]
        head_mixed = bank[2][:, 0:D]
        scores_sb, adj_sb = raw[:, 0, :], raw[:, 1, :]

        def needed(eng):
            eng.wait_ge(flag_step, FLAG_STEPS)
            return eng.value_load(flag_int[0:1, 0:1], min_val=0, max_val=2 * N * N + 1) >= 1

        def heads_and_tiles(eng, per_head, per_tile):
            with eng.Fori(0, HEADS) as h:
                per_head(h)
                with eng.Fori(0, TILES) as t:
                    per_tile(h * TILES + t, t)

        def operand_tiles(t, s):
            if not isinstance(t, int) or t > HELD + 2:
                return [(t - Z_LAG, (s - Z_LAG) % 4)]
            return [(v, v) for v in {HELD: (0,), HELD + 1: (1,), HELD + 2: (2, 3)}.get(t, ())]

        def next_split(t, s):
            if not isinstance(t, int) or HELD + 2 <= t < TILES:
                return [(t - HELD, s, q) for q in range(CHUNKS)]
            return [(0, 0, q) for q in range(CHUNKS)] if t == 0 else [None] * CHUNKS

        def late_split(t):
            return [(1, 1, q) for q in range(CHUNKS) if t == q + 1] if isinstance(t, int) else []

        def score_order(u):
            return (0, 2, 1, 3) if isinstance(u, int) and u == 0 else range(CHUNKS)

        block = ctx.enter_context(nc.Block())

        later_weights = ((wqT_sb[:, :, :], wqT), (wkT_sb[:, :, :], wkT), (wvT_sb[:, :, :], wvT),
                         (bq_sb[:, :], bq), (bk_sb[:, :], bk), (bv_sb[:, :], bv), (diag[:, :], adj_diag))

        @block.sync
        def _(sp):
            def rows(t, s):
                wait(sp, row_summed, t - 3)
                wait(sp, row_counted, t - 3)
                held = isinstance(t, int) and t < HELD
                sp.dma_start(row_slot[s], (adjT if held else adj)[tile_cols(t), :]).then_inc(row_in[s], 16)

            over_tiles(sp, rows, peel=4, slots=4)

            def blocks0(n, s):
                if isinstance(n, int) and n < 2:
                    sp.wait_ge(row_summed, TILES - 3 + n)
                    sp.wait_ge(row_counted, TILES - 3 + n)
                wait(sp, L0["lo"], (n - 1) * CHUNKS)
                sp.dma_start(raw[:, s, :], adjT[tile_cols(n + HELD), :]).then_inc(L0[f"in{s}"], 16)
                if isinstance(n, int) and n < 2:
                    sp.wait_ge(row_summed, TILES - 1 + n)
                    sp.wait_ge(row_counted, TILES - 1 + n)
                    half = slice(n * TILES // 2, (n + 1) * TILES // 2)
                    sp.dma_start(X[:, half, :], x[:, half, :]).then_inc(x_in[n], 16)
                if isinstance(n, int) and n == 1:
                    for dst, src in later_weights:
                        sp.dma_start(dst, src).then_inc(w_in, 16)

            over_tiles(sp, blocks0, count=TILES - HELD)

            def blocks1(t, s):
                if isinstance(t, int) and t < 2:
                    sp.wait_ge(L0["lo"], (TILES - HELD - 1 + t) * CHUNKS)
                wait(sp, L1["lo"], (t - 1) * CHUNKS)
                wait(sp, L1["edges"], (t - 1) * CHUNKS)
                wait(sp, L1["signs"], t - 1)
                sp.dma_start(raw[:, s, :], adjT[tile_cols(t), :]).then_inc(L1[f"in{s}"], 16)

            over_tiles(sp, blocks1)

            def attention(t, s):
                if active(t, 4):
                    u = t - 4
                    sp.wait_ge(L2["out"], u + 1)
                    sp.dma_start(out[tile_cols(u), :], out_tile[:, s, :]).then_inc(L2[f"stored{s}"], 16)
                if active(t, 0):
                    if isinstance(t, int) and t < 2:
                        sp.wait_ge(L1["lo"], (TILES - 1 + t) * CHUNKS)
                        sp.wait_ge(L1["edges"], (TILES - 1 + t) * CHUNKS)
                    wait(sp, L2["tr_ps"], (t - 1) * CHUNKS)
                    sp.dma_start(raw[:, s, :], adj[tile_cols(t), :]).then_inc(L2[f"in{s}"], 16)

            over_tiles(sp, attention, lag=4, peel=4)
            for s in range(2):
                sp.wait_ge(L2[f"stored{s}"], 16 * TILES // 2)

            with sp.If(needed(sp)):
                def weights(h):
                    sp.wait_ge(G["added"], h * TILES + 1)
                    for dst, src in ((head_wq, hwq), (head_wk, hwk), (head_wv, hwv)):
                        sp.dma_start(dst, src.rearrange("p (c h k) -> p c h k", c=DC, h=HEADS)[:, :, h, :])\
                            .then_inc(G["weights"], 16)
                    sp.dma_start(head_wo, hwo_rows[bass.ds(h * KD, KD), :]).then_inc(G["weights"], 16)

                def adjacency(n, t):
                    sp.wait_ge(G["taken"], n + 1)
                    sp.dma_start(adj_sb, adj[tile_cols(t), :]).then_inc(G["adj_in"], 16)

                heads_and_tiles(sp, weights, adjacency)
                with sp.Fori(0, TILES // 2) as pair:
                    for s in range(2):
                        sp.wait_ge(G["normed"], pair * 2 + s + 1)
                        sp.dma_start(out[tile_cols(pair * 2 + s), :], out_tile[:, s, :])\
                            .then_inc(G[f"stored{s}"], 16)
                for s in range(2):
                    sp.wait_ge(G[f"stored{s}"], 16 * TILES // 2 + 16)

        @block.gpsimd
        def _(pool):
            nc.gpsimd.memset(minus_half[:, :], -0.5).then_inc(consts, 1)
            nc.gpsimd.memset(ones[:, :], 1.0).then_inc(consts, 1)
            nc.gpsimd.memset(sums[:, :], 0.0).then_inc(consts, 1)
            nc.gpsimd.memset(ln_eps[:, :], LN_EPS).then_inc(consts, 1)
            nc.gpsimd.memset(below_one[:, :], -(1.0 - 2.0 ** -24)).then_inc(consts, 1)
            pool.wait_ge(consts, 5)

            def degree(t, s):
                one = bass.ds(t, 1)
                if isinstance(t, int) and t < HELD:
                    pool.wait_ge(held_taken, t + 1)
                else:
                    pool.wait_ge(row_summed, t + 1)
                nc.gpsimd.tensor_tensor(deg1[:, one], deg[:, one], ones[:, 0:1], ALU.add).then_inc(deg1_done, 1)
                pool.wait_ge(deg1_done, t + 1)
                nc.gpsimd.tensor_tensor(dinv[:, one], deg1[:, one], minus_half[:, 0:1], ALU.pow)\
                    .then_inc(dinv_done, 1)

            over_tiles(pool, degree, peel=HELD)
            pool.wait_ge(degree_step, 1)
            nc.gpsimd.tensor_tensor(rcount[:, :], count_safe[:, :], minus_half[:, :], ALU.pow)\
                .then_inc(rcount_done, 1)

            def norm_scale(L, t, s):
                pool.wait_ge(L["mv"], t + 1)
                nc.gpsimd.tensor_tensor(veps[:, s, :], mv[:, s, 1:2], ln_eps[:, :], ALU.add).then_inc(L["veps"], 1)
                pool.wait_ge(L["veps"], t + 1)
                nc.gpsimd.tensor_tensor(rstd[:, s, :], veps[:, s, :], minus_half[:, 0:1], ALU.pow)\
                    .then_inc(L["rstd"], 1)

            def keep_rows(L, t, s):
                pool.wait_ge(L["xn"], t + 1)
                nc.gpsimd.tensor_copy(X[:, t, :], xn[:, s, :]).then_inc(L["rows"], 1)

            def step0(t, s):
                norm_scale(L0, t, s)
                keep_rows(L0, t, s)

            over_tiles(pool, step0)

            def step1(t, s):
                norm_scale(L1, t, s)
                keep_rows(L1, t, s)
                pool.wait_ge(L1["xT"], t + 1)
                nc.gpsimd.tensor_copy(XT[:, :, tile_cols(t)], xT_tile[:, s, :, :]).then_inc(L1["xT_all"], 1)

            over_tiles(pool, step1)

            def step2(t, s):
                if active(t, 1):
                    u = t - 1
                    pool.wait_ge(L2["mv3"], u + 1)
                    nc.gpsimd.tensor_tensor(veps3[:, :], mv3[:, 1:2], ln_eps[:, :], ALU.add)\
                        .then_inc(L2["veps3"], 1)
                    pool.wait_ge(L2["veps3"], u + 1)
                    nc.gpsimd.tensor_tensor(rstd3[:, :], veps3[:, :], minus_half[:, 0:1], ALU.pow)\
                        .then_inc(L2["rstd3"], 1)
                if active(t, 0):
                    norm_scale(L2, t, s)
                    keep_rows(L2, t, s)

                if active(t, 1):
                    u = t - 1
                    pool.wait_ge(L2["xT"], u + 1)
                    nc.gpsimd.tensor_copy(XT[:, :, tile_cols(u)], xT_tile[:, 1 - s, :, :]).then_inc(L2["xT_all"], 1)

            over_tiles(pool, step2, lag=1)

            with pool.If(needed(pool)):
                with pool.Fori(0, TILES) as t:
                    pool.wait_ge(G["mv"], t + 1)
                    nc.gpsimd.tensor_tensor(veps3[:, :], mv3[:, 1:2], ln_eps[:, :], ALU.add).then_inc(G["veps"], 1)
                    pool.wait_ge(G["veps"], t + 1)
                    nc.gpsimd.tensor_tensor(rstd3[:, :], veps3[:, :], minus_half[:, 0:1], ALU.pow)\
                        .then_inc(G["rstd"], 1)

        @block.scalar
        def _(act):
            for s, src in ((0, hwvT), (1, hwo)):
                act.dma_start(stage[:, s, :], src).then_inc(stage_vo_in, 16)
            for dst, src in ((w0_sb[:, :, :], w0), (XT[:, :, :], xT)):
                act.dma_start(dst, src).then_inc(xT_in, 16)
            act.dma_start(ident[:, :], ident_in).then_inc(ident_in_sem, 16)

            act.wait_ge(consts, 5)
            nc.scalar.activation(ones_r[:, :], ones[:, 0:1], ACT.Copy).then_inc(ones_ready, 1)

            def degree(t, s):
                if isinstance(t, int) and t < HELD:
                    act.wait_ge(row_in[s], loaded(t, s, 4))
                    nc.scalar.activation(held_hi[t], row_slot[s], ACT.Copy).then_inc(row_summed, 1)
                elif active(t, 0):
                    act.wait_ge(row_in[s], loaded(t, s, 4))
                    wait(act, row_summed, t)
                    nc.scalar.activation(sign_out[:, :], row_slot[s], ACT.Copy,
                                         accum_out=deg[:, bass.ds(t, 1)]).then_inc(row_summed, 1)
                if isinstance(t, int) and t == HELD - 1:
                    act.wait_ge(wvo_ps, DC)
                    for c in range(DC):
                        nc.scalar.activation(wvo_sb[:, c, :], wvo_out[c], ACT.Copy).then_inc(wvo_ready, 1)
                    act.wait_ge(ident_in_sem, 16)
                    nc.scalar.activation(ident_r[:, :], ident[:, :], ACT.Copy).then_inc(ident_ready, 1)
                for v, slot in operand_tiles(t, s):
                    act.wait_ge(dinv_done, v + 1)
                    act.wait_ge(xw_done, v + 1)
                    nc.scalar.activation(opA_hi[:, v, :], xw_out[slot], ACT.Copy,
                                         scale=dinv[:, bass.ds(v, 1)]).then_inc(z_hi, 1)

            over_tiles(act, degree, lag=Z_LAG, peel=8, slots=4)
            act.wait_ge(row_summed, TILES)

            def weight_norms():
                act.wait_ge(L1["signs"], 4)
                act.wait_ge(stage_qk_in, 32)
                for s in range(2):
                    wait(act, norms_done, s)
                    nc.scalar.activation(sign_out[:, 0:HK * DC], stage[:, s, :], ACT.Square,
                                         accum_out=sums[:, 1 + s:2 + s]).then_inc(norms_done, 1)
                act.wait_ge(norms_done, 2)

            def split_hi(L, t, s, q):
                if q == 0:
                    act.wait_ge(L[f"in{s}"], loaded(t, s))
                if L is L1 and isinstance(t, int) and t == 0:
                    act.wait_ge(L0["chunk_used"], (TILES - HELD - 1) * CHUNKS + q + 1)
                wait(act, L["chunk_used"], (t - 1) * CHUNKS + q + 1)
                nc.scalar.activation(part_hi[:, q, :], raw[:, s, q * BLK:(q + 1) * BLK], ACT.Copy)\
                    .then_inc(L["hi"], 1)

            def step0(t, s):
                for chunk in next_split(t, s):
                    if chunk:
                        split_hi(L0, *chunk)
                if isinstance(t, int) and 1 <= t <= HELD:
                    u = t - 1
                    act.wait_ge(L0["acc"], u + 1)
                    wait(act, L0["y"], u)
                    nc.scalar.activation(branch[:, :], held_acc[u], ACT.Relu, scale=dinv[:, u:u + 1])\
                        .then_inc(L0["branch"], 1)
                for chunk in late_split(t):
                    split_hi(L0, *chunk)
                if isinstance(t, int) and t == TILES:
                    for q in range(CHUNKS - 1):
                        split_hi(L1, 0, 0, q)
                if active(t, 2):
                    v = t - 2
                    if isinstance(t, int) and t == 2:
                        act.wait_ge(L0["acc"], HELD)
                    act.wait_ge(L0["xn"], v + 1)
                    nc.scalar.activation(opB_hi[:, v, :], xn[:, s, :], ACT.Copy).then_inc(L0["op_hi"], 1)
                if isinstance(t, int) and t == 1:
                    act.wait_ge(wvo_ready, DC)
                    for k, src in ((0, hwq), (1, hwk)):
                        act.dma_start(stage[:, k, :], src).then_inc(stage_qk_in, 16)
                if isinstance(t, int) and t == TILES:
                    split_hi(L1, 0, 0, CHUNKS - 1)

            over_tiles(act, step0, lag=2, peel=HELD + 2)

            act.wait_ge(w_in, 16 * len(later_weights))

            def queries_hi(t):
                act.wait_ge(L2["qf"], DC * (t + 1))
                wait(act, L2["scores"], t * CHUNKS)
                nc.scalar.activation(q_hi[:, :, :], qf[:, :, :], ACT.Copy).then_inc(L2["q_hi"], 1)

            def step1(t, s):
                for q in range(CHUNKS):
                    if active(t, 0) and not (isinstance(t, int) and t == 0):
                        split_hi(L1, t, s, q)
                    if q == 1 and isinstance(t, int) and t == TILES + 1:
                        queries_hi(0)
                    if q == 0 and active(t, 3):
                        w = t - 3
                        act.wait_ge(L1["xT_ps"], w + 1)
                        wait(act, L1["value_ps"], w - 1)
                        wait(act, L1["xT_all"], w - 1)
                        nc.scalar.activation(xT_tile[:, 1 - s, :, :], xT_out1, ACT.Copy).then_inc(L1["xT"], 1)
                    if q == 1 and active(t, 0):
                        wait(act, L1["signs"], t)
                        nc.scalar.activation(sign_out[:, :], raw[:, s, :], ACT.Sign, bias=below_one[:, :],
                                             accum_out=signs[:, bass.ds(t, 1)]).then_inc(L1["signs"], 1)
                    if q == 2 and active(t, 3):
                        w = t - 3
                        act.wait_ge(L1["key_ps"], w + 1)
                        for c in range(DC):
                            nc.scalar.activation(keyT_hi[:, c, tile_cols(w)], key_out[:, c, :], ACT.Identity,
                                                 bias=bk_sb[:, c:c + 1]).then_inc(L1["key_hi"], 1)
                        act.wait_ge(L1["value"], w + 1)
                        nc.scalar.activation(opA_hi[:, w, :], vf[:, :], ACT.Copy).then_inc(L1["value_hi"], 1)
                if isinstance(t, int) and t == 3:
                    weight_norms()
                if active(t, 1):
                    u = t - 1
                    act.wait_ge(L1["chunk_used"], (u + 1) * CHUNKS)
                    wait(act, L1["sum"], u)
                    nc.scalar.activation(branch[:, :], acc_edges[1 - s], ACT.Copy,
                                         scale=rcount[:, bass.ds(u, 1)]).then_inc(L1["branch"], 1)

            over_tiles(act, step1, lag=3, peel=4)

            def weights_hi(u, q):
                act.wait_ge(L2["tr_ps"], u * CHUNKS + q + 1)
                wait(act, L2["attended"], (u - 1) * CHUNKS + q + 1)
                nc.scalar.activation(part_hi[:, q, :], bank[q % 2][:, :], ACT.Copy).then_inc(L2["w_hi"], 1)

            def step2(t, s):
                if active(t, 2):
                    weights_hi(t - 2, 0)
                    weights_hi(t - 2, 1)
                if isinstance(t, int) and t == 1:
                    queries_hi(1)
                if active(t, 1):
                    u = t - 1
                    act.wait_ge(L2["nmax"], u + 1)
                    wait(act, L2["rsum"], u - 1)
                    nc.scalar.activation(raw[:, 1 - s, :], raw[:, 1 - s, :], ACT.Exp, bias=nmax[:, 1 - s, :],
                                         accum_out=wsum[:, 1 - s, :]).then_inc(L2["exp"], 1)
                if active(t, 0) and not (isinstance(t, int) and t < 2):
                    queries_hi(t)
                if active(t, 2):
                    weights_hi(t - 2, 2)
                if active(t, 3):
                    u = t - 3
                    act.wait_ge(L2["xT_ps"], u + 1)
                    wait(act, L2["mixed"], u - 1)
                    wait(act, L2["xT_all"], u - 1)
                    act.wait_ge(L2["qf"], DC * (t + 1) if active(t, 0) else DC * TILES)
                    nc.scalar.activation(xT_tile[:, 1 - s, :, :], xT_out2, ACT.Copy).then_inc(L2["xT"], 1)
                if active(t, 2):
                    weights_hi(t - 2, 3)

            over_tiles(act, step2, lag=3, peel=4)

            with act.If(needed(act)):
                def head_operands(h):
                    act.wait_ge(G["key_ps"], h + 1)
                    nc.scalar.activation(head_key_hi, head_key_out, ACT.Copy).then_inc(G["key_hi"], 1)
                    act.wait_ge(G["value_ps"], h + 1)
                    for k in range(2):
                        nc.scalar.activation(head_value_hi[:, k * TILES // 2:(k + 1) * TILES // 2, :],
                                             head_value_out[k], ACT.Copy).then_inc(G["value_hi"], 1)

                def tile(n, t):
                    act.wait_ge(G["qf"], n + 1)
                    nc.scalar.activation(head_q_hi, head_qf, ACT.Copy).then_inc(G["q_hi"], 1)
                    act.wait_ge(G["mx"], 2 * n + 2)
                    nc.scalar.activation(scores_sb, scores_sb, ACT.Exp, bias=nmax[:, 0, :],
                                         accum_out=wsum[:, 0, :]).then_inc(G["exp"], 1)
                    for q in range(CHUNKS):
                        act.wait_ge(G["tr_ps"], n * CHUNKS + q + 1)
                        nc.scalar.activation(part_hi[:, q, :], bank[q % 2][:, :], ACT.Copy).then_inc(G["w_hi"], 1)
                    act.wait_ge(G["head_t_ps"], n + 1)
                    nc.scalar.activation(head_T, head_T_out, ACT.Copy).then_inc(G["head_t"], 1)

                heads_and_tiles(act, head_operands, tile)

        @block.vector
        def _(dve):
            def held_to_row(r):
                dve.wait_ge(held_summed, r + 1)
                nc.vector.tensor_reduce(out=held_rows, in_=held_rows_out.rearrange("p w (k i) -> p w i k", i=P),
                                        axis=AX.X, op=ALU.add).then_inc(held_row, 1)

            def held_to_columns(r):
                dve.wait_ge(held_column, r + 1)
                nc.vector.tensor_copy(deg_count[:, :, r], held_columns).then_inc(held_taken, 1)

            def degree(t, s):
                if isinstance(t, int) and t < HELD:
                    dve.wait_ge(row_summed, t + 1)
                    nc.vector.tensor_tensor(held_lo[t], row_slot[s], f32(held_hi[t]), ALU.subtract)\
                        .then_inc(held_lo_done, 1)
                    if t > 0:
                        held_to_row(t - 1)
                    nc.vector.tensor_scalar(edges_flat, row_slot[s], 0.0, None, ALU.is_gt).then_inc(row_counted, 1)
                elif active(t, 0):
                    dve.wait_ge(row_in[s], loaded(t, s, 4))
                    wait(dve, row_counted, t)
                    nc.vector.tensor_scalar(part_lo[:, :, :].rearrange("p q n -> p (q n)"), row_slot[s], 0.0, 0.0,
                                            ALU.is_gt, ALU.add, accum_out=count[:, bass.ds(t, 1)])\
                        .then_inc(row_counted, 1)
                if isinstance(t, int) and 1 <= t < HELD:
                    held_to_columns(t - 1)
                if isinstance(t, int) and t == HELD:
                    held_to_row(t - 1)
                    held_to_columns(t - 1)
                for v, slot in operand_tiles(t, s):
                    dve.wait_ge(z_hi, v + 1)
                    nc.vector.scalar_tensor_tensor(opA_lo[:, v, :], xw_out[slot], dinv[:, bass.ds(v, 1)],
                                                   f32(opA_hi[:, v, :]), ALU.mult, ALU.subtract).then_inc(z_lo, 1)

            over_tiles(dve, degree, lag=Z_LAG, peel=8, slots=4)
            dve.wait_ge(row_counted, TILES)
            nc.vector.tensor_scalar(count_safe[:, :], count[:, :], EDGE_EPS ** 2, None, ALU.max)\
                .then_inc(degree_step, 1)

            def split_lo(L, t, s, q):
                dve.wait_ge(L["hi"], t * CHUNKS + q + 1)
                nc.vector.tensor_tensor(part_lo[:, q, :], raw[:, s, q * BLK:(q + 1) * BLK], f32(part_hi[:, q, :]),
                                        ALU.subtract).then_inc(L["lo"], 1)

            def statistics(L, u, b):
                dve.wait_ge(L["y"], u + 1)
                nc.vector.bn_stats(stats[:, b, :], ysum[:, b, :]).then_inc(L["stats"], 1)
                dve.wait_ge(L["stats"], u + 1)
                wait(dve, L["rstd"], u - 1)
                own_instruction(dve, dve_held)
                nc.vector.bn_aggr(mv[:, b, :], stats[:, b, :]).then_inc(L["mv"], 1)

            def norm(L, u, b):
                dve.wait_ge(L["rstd"], u + 1)
                wait(dve, L["rows"], u - 1)
                nc.vector.tensor_scalar(xn[:, b, :], ysum[:, b, :], mv[:, b, 0:1], rstd[:, b, :],
                                        ALU.subtract, ALU.mult).then_inc(L["xn"], 1)

            def take_edges(t, s, q):
                nc.vector.tensor_scalar(edges[:, q, :], raw[:, s, q * BLK:(q + 1) * BLK], 0.0, None, ALU.is_gt)\
                    .then_inc(L1["edges"], 1)

            def step0(t, s):
                for q, chunk in enumerate(next_split(t, s)):
                    if chunk:
                        split_lo(L0, *chunk)
                    if q == 0 and active(t, 3):
                        w = t - 3
                        dve.wait_ge(L0["op_hi"], w + 1)
                        nc.vector.tensor_tensor(opB_lo[:, w, :], xn[:, 1 - s, :], f32(opB_hi[:, w, :]), ALU.subtract)\
                            .then_inc(L0["op_lo"], 1)
                    if q == 1 and active(t, 2):
                        v = t - 2
                        wait(dve, L0["op_hi"], v - 1)
                        wait(dve, L0["op_lo"], v - 1)
                        norm(L0, v, s)
                    if isinstance(t, int) and t == TILES and q < CHUNKS - 1:
                        split_lo(L1, 0, 0, q)
                        take_edges(0, 0, q)
                if active(t, 1):
                    b, u = 1 - s, t - 1
                    if not (isinstance(u, int) and u < HELD):
                        dve.wait_ge(L0["acc"], u + 1)
                        wait(dve, L0["y"], u)
                        nc.vector.tensor_scalar(branch[:, :], acc_weighted[b], dinv[:, bass.ds(u, 1)], 0.0,
                                                ALU.mult, ALU.max).then_inc(L0["branch"], 1)
                    if isinstance(t, int) and t == 1:
                        dve.wait_ge(x_in[0], 16)
                    if isinstance(t, int) and t == HELD + 1:
                        dve.wait_ge(x_in[1], 16)
                    dve.wait_ge(L0["branch"], u + 1)
                    nc.vector.tensor_tensor(ysum[:, b, :], branch[:, :], X[:, u, :], ALU.add).then_inc(L0["y"], 1)
                    statistics(L0, u, b)
                for chunk in late_split(t):
                    split_lo(L0, *chunk)
                if isinstance(t, int) and t == TILES:
                    split_lo(L1, 0, 0, CHUNKS - 1)
                    take_edges(0, 0, CHUNKS - 1)

            over_tiles(dve, step0, lag=3, peel=HELD + 2)

            dve.wait_ge(rcount_done, 1)
            nc.vector.tensor_tensor(head_sum[:, :], count[:, :], rcount[:, :], ALU.mult).then_inc(degree_step, 1)
            dve.wait_ge(degree_step, 2)
            nc.vector.tensor_tensor(edge_deg[:, :], head_sum[:, :], deg[:, :], ALU.add).then_inc(degree_step, 1)
            dve.wait_ge(degree_step, 3)
            nc.vector.reciprocal(redge[:, :], edge_deg[:, :]).then_inc(degree_step, 1)

            dve.wait_ge(w_in, 16 * len(later_weights))

            def full_edges():
                dve.wait_ge(L1["signs"], TILES)
                nc.vector.tensor_scalar(diag_sign[:, :], diag[:, :], 1.0 - 2.0 ** -24, None, ALU.is_gt)\
                    .then_inc(flag_step, 1)
                nc.vector.tensor_scalar(diag_least[:, :], diag[:, :], 1.0 - 2.0 ** -24, None, ALU.is_ge)\
                    .then_inc(flag_step, 1)
                dve.wait_ge(flag_step, 2)
                nc.vector.tensor_tensor(diag_sign[:, :], diag_sign[:, :], diag_least[:, :], ALU.add)\
                    .then_inc(flag_step, 1)
                dve.wait_ge(flag_step, 3)
                nc.vector.tensor_tensor(signs[:, :], signs[:, :], diag_sign[:, :], ALU.subtract).then_inc(flag_step, 1)
                dve.wait_ge(flag_step, 4)
                nc.vector.tensor_scalar(signs[:, :], signs[:, :], float(N), None, ALU.add).then_inc(flag_step, 1)
                dve.wait_ge(flag_step, 5)
                nc.vector.reduce_sum(sums[:, 0:1], signs[:, :], axis=AX.X).then_inc(flag_step, 1)

            def mask_scores(u, b, n, q):
                dve.wait_ge(L2["scores"], u * CHUNKS + n + 1)
                own_instruction(dve, dve_held)
                part = raw[:, b, q * BLK:(q + 1) * BLK]
                nc.vector.tensor_tensor_reduce(out=part, in0=wide[:, q, :], in1=part, scale=2.0,
                                               scalar=LOWEST, op0=ALU.add, op1=ALU.max,
                                               accum_out=mx[:, q:q + 1]).then_inc(L2["masked"], 1)

            def queries(t):
                dve.wait_ge(L2["q_ps"], t + 1)
                wait(dve, L2["q_hi"], t)
                wait(dve, L2["q_lo"], t)
                for c in range(DC):
                    nc.vector.tensor_scalar(qf[:, c, :], q_out[:, c, :], bq_sb[:, c:c + 1], ATT_SCALE / 2,
                                            ALU.add, ALU.mult).then_inc(L2["qf"], 1)

            def queries_lo(t):
                dve.wait_ge(L2["q_hi"], t + 1)
                nc.vector.tensor_tensor(q_lo[:, :, :], qf[:, :, :], f32(q_hi[:, :, :]), ALU.subtract)\
                    .then_inc(L2["q_lo"], 1)

            def step1(t, s):
                if isinstance(t, int) and t == TILES + 1:
                    queries(0)
                for q in range(CHUNKS):
                    if active(t, 0) and not (isinstance(t, int) and t == 0):
                        split_lo(L1, t, s, q)
                        take_edges(t, s, q)
                    if q == 1 and isinstance(t, int) and t == TILES + 1:
                        queries_lo(0)
                        full_edges()
                    if q == 1 and isinstance(t, int) and t == TILES + 2:
                        dve.wait_ge(L2["in0"], 16)
                        for n, chunk in enumerate(score_order(0)[:3]):
                            mask_scores(0, 0, n, chunk)
                        queries(1)
                    if q == 0 and active(t, 2):
                        wait(dve, L1["xT_ps"], t - 3)
                        norm(L1, t - 2, s)
                    if q == 2 and active(t, 3):
                        w = t - 3
                        dve.wait_ge(L1["value_ps"], w + 1)
                        wait(dve, L1["value_hi"], w)
                        wait(dve, L1["value_lo"], w)
                        nc.vector.tensor_tensor(vf[:, :], value_out, bv_sb[:, :], ALU.add).then_inc(L1["value"], 1)
                        dve.wait_ge(L1["key_hi"], DC * w + DC)
                        for c in range(DC):
                            nc.vector.scalar_tensor_tensor(keyT_lo[:, c, tile_cols(w)], key_out[:, c, :],
                                                           bk_sb[:, c:c + 1], f32(keyT_hi[:, c, tile_cols(w)]),
                                                           ALU.add, ALU.subtract).then_inc(L1["key_lo"], 1)
                        dve.wait_ge(L1["value_hi"], w + 1)
                        nc.vector.tensor_tensor(opA_lo[:, w, :], vf[:, :], f32(opA_hi[:, w, :]), ALU.subtract)\
                            .then_inc(L1["value_lo"], 1)
                if active(t, 1):
                    b, u = 1 - s, t - 1
                    dve.wait_ge(L1["branch"], u + 1)
                    nc.vector.tensor_tensor(ysum[:, b, :], acc_weighted[b], branch[:, :], ALU.add)\
                        .then_inc(L1["sum"], 1)
                    dve.wait_ge(L1["sum"], u + 1)
                    nc.vector.scalar_tensor_tensor(ysum[:, b, :], ysum[:, b, :], redge[:, bass.ds(u, 1)],
                                                   X[:, u, :], ALU.mult, ALU.add).then_inc(L1["y"], 1)
                    statistics(L1, u, b)

            over_tiles(dve, step1, lag=3, peel=4)

            def needs_general_path():
                dve.wait_ge(totals_done, 1)
                nc.vector.tensor_copy(flag[0:1, 0:4], totals).then_inc(flag_step, 1)
                dve.wait_ge(flag_step, 7)
                nc.vector.tensor_tensor(flag[0:1, 4:5], flag[0:1, 1:2], flag[0:1, 2:3], ALU.mult)\
                    .then_inc(flag_step, 1)
                dve.wait_ge(flag_step, 8)
                nc.vector.tensor_scalar(flag[0:1, 5:6], flag[0:1, 4:5], NORMS_BOUND, None, ALU.is_ge)\
                    .then_inc(flag_step, 1)
                dve.wait_ge(flag_step, 9)
                nc.vector.tensor_tensor(flag_int[0:1, :], flag[0:1, 0:1], flag[0:1, 5:6], ALU.add)\
                    .then_inc(flag_step, 1)

            def weights_lo(u, q):
                dve.wait_ge(L2["w_hi"], u * CHUNKS + q + 1)
                nc.vector.tensor_tensor(part_lo[:, q, :], bank[q % 2][:, :], f32(part_hi[:, q, :]),
                                        ALU.subtract).then_inc(L2["w_lo"], 1)

            def step2(t, s):
                if isinstance(t, int) and t == 2:
                    needs_general_path()
                def layer3_sum(u):
                    dve.wait_ge(L2["mixed"], u + 1)
                    nc.vector.tensor_tensor(y3[:, :], mixed_of(u), xn[:, s, :], ALU.add).then_inc(L2["y3"], 1)
                    dve.wait_ge(L2["y3"], u + 1)
                    nc.vector.bn_stats(stats3[:, :], y3[:, :]).then_inc(L2["stats3"], 1)
                    dve.wait_ge(L2["stats3"], u + 1)
                    own_instruction(dve, dve_held)
                    nc.vector.bn_aggr(mv3[:, :], stats3[:, :]).then_inc(L2["mv3"], 1)

                def layer2_sum(u, b):
                    dve.wait_ge(L2["attended"], (u + 1) * CHUNKS)
                    dve.wait_ge(L2["exp"], u + 1)
                    nc.vector.reciprocal(rsum[:, :], wsum[:, b, :]).then_inc(L2["rsum"], 1)
                    dve.wait_ge(L2["rsum"], u + 1)
                    nc.vector.scalar_tensor_tensor(ysum[:, b, :], attended, rsum[:, :], X[:, u, :],
                                                   ALU.mult, ALU.add).then_inc(L2["y"], 1)

                last_weights = isinstance(t, int) and t == TILES + 1
                if active(t, 4) and not last_weights:
                    layer3_sum(t - 4)
                if active(t, 3):
                    layer2_sum(t - 3, 1 - s)
                if last_weights:
                    weights_lo(t - 2, 0)
                    weights_lo(t - 2, 1)
                if active(t, 3):
                    statistics(L2, t - 3, 1 - s)
                if last_weights:
                    layer3_sum(t - 4)
                if active(t, 4):
                    u = t - 4
                    dve.wait_ge(L2["rstd3"], u + 1)
                    wait(dve, L2[f"stored{s}"], (u - s) * 8)
                    nc.vector.tensor_scalar(out_tile[:, s, :], y3[:, :], mv3[:, 0:1], rstd3[:, :],
                                            ALU.subtract, ALU.mult).then_inc(L2["out"], 1)
                if active(t, 1):
                    b, u = 1 - s, t - 1
                    dve.wait_ge(L2[f"in{b}"], loaded(u, b))
                    wait(dve, L2["mx"], u)
                    for n, q in enumerate(score_order(u)):
                        if not (isinstance(t, int) and t == 1 and n < 3):
                            mask_scores(u, b, n, q)
                        if n == 1 and active(t, 3):
                            norm(L2, t - 3, b)
                    if isinstance(t, int) and t == 1:
                        queries_lo(1)
                    dve.wait_ge(L2["masked"], (u + 1) * CHUNKS)
                    wait(dve, L2["exp"], u - 1)
                    nc.vector.reduce_max(nmax[:, b, :], mx[:, :], axis=AX.X).then_inc(L2["mx"], 1)
                    dve.wait_ge(L2["mx"], u + 1)
                    nc.vector.tensor_scalar(nmax[:, b, :], nmax[:, b, :], -1.0, None, ALU.mult)\
                        .then_inc(L2["nmax"], 1)
                elif active(t, 3):
                    norm(L2, t - 3, 1 - s)
                if active(t, 2) and not last_weights:
                    weights_lo(t - 2, 0)
                    weights_lo(t - 2, 1)
                if active(t, 0) and not (isinstance(t, int) and t < 2):
                    queries(t)
                    queries_lo(t)
                if active(t, 2):
                    weights_lo(t - 2, 2)
                    weights_lo(t - 2, 3)

            over_tiles(dve, step2, lag=4, peel=4)

            with dve.If(needed(dve)):
                dve.wait_ge(L2["out"], TILES)
                dve.wait_ge(L2["xT_all"], TILES)
                dve.wait_ge(L2["stored0"], 16 * TILES // 2)
                dve.wait_ge(L2["stored1"], 16 * TILES // 2)
                nc.vector.memset(head_padded[:, :], 0.0).then_inc(G["zeroed"], 1)
                dve.wait_ge(G["zeroed"], 1)
                nc.vector.memset(mx[:, :], 0.0).then_inc(G["taken"], 1)
                dve.wait_ge(G["taken"], 1)
                nc.vector.memset(mx[:, :], 0.0).then_inc(G["added"], 1)

                def head_operands(h):
                    dve.wait_ge(G["key_hi"], h + 1)
                    nc.vector.tensor_tensor(head_key_lo, head_key_out.rearrange("p q n -> p (q n)"), f32(head_key_hi),
                                            ALU.subtract).then_inc(G["key_lo"], 1)
                    dve.wait_ge(G["value_hi"], h * 2 + 2)
                    for k in range(2):
                        part = slice(k * TILES // 2, (k + 1) * TILES // 2)
                        nc.vector.tensor_tensor(head_value_lo[:, part, :], head_value_out[k],
                                                f32(head_value_hi[:, part, :]), ALU.subtract)\
                            .then_inc(G["value_lo"], 1)

                def tile(n, t):
                    dve.wait_ge(G["q_ps"], n + 1)
                    nc.vector.tensor_scalar(head_qf, head_q_out, HEAD_SCALE, None, ALU.mult).then_inc(G["qf"], 1)
                    dve.wait_ge(G["q_hi"], n + 1)
                    nc.vector.tensor_tensor(head_q_lo, head_qf, f32(head_q_hi), ALU.subtract).then_inc(G["q_lo"], 1)
                    dve.wait_ge(G["adj_in"], n * 16 + 16)
                    on_diagonal = adj_sb[:, tile_cols(t)]
                    nc.vector.tensor_tensor(on_diagonal, on_diagonal, ident[:, :], ALU.max).then_inc(G["penalty"], 1)
                    dve.wait_ge(G["penalty"], 2 * n + 1)
                    nc.vector.tensor_scalar(adj_sb, adj_sb, -1.0, 1.0, ALU.mult, ALU.add).then_inc(G["penalty"], 1)
                    dve.wait_ge(G["scores"], n + 1)
                    dve.wait_ge(G["penalty"], 2 * n + 2)
                    nc.vector.scalar_tensor_tensor(scores_sb, adj_sb, -MASK_VAL,
                                                   wide[:, :, :].rearrange("p q n -> p (q n)"),
                                                   ALU.mult, ALU.add).then_inc(G["taken"], 1)
                    dve.wait_ge(G["taken"], n + 2)
                    on_diagonal = scores_sb[:, tile_cols(t)]
                    nc.vector.scalar_tensor_tensor(on_diagonal, ident[:, :], IDENTITY_BIAS, on_diagonal,
                                                   ALU.mult, ALU.add).then_inc(G["masked"], 1)
                    dve.wait_ge(G["masked"], n + 1)
                    nc.vector.reduce_max(nmax[:, 1, :], scores_sb, axis=AX.X).then_inc(G["mx"], 1)
                    dve.wait_ge(G["mx"], 2 * n + 1)
                    nc.vector.tensor_scalar(nmax[:, 0, :], nmax[:, 1, :], -1.0, None, ALU.mult).then_inc(G["mx"], 1)
                    for q in range(CHUNKS):
                        dve.wait_ge(G["w_hi"], n * CHUNKS + q + 1)
                        nc.vector.tensor_tensor(part_lo[:, q, :], bank[q % 2][:, :], f32(part_hi[:, q, :]),
                                                ALU.subtract).then_inc(G["w_lo"], 1)
                    dve.wait_ge(G["exp"], n + 1)
                    nc.vector.reciprocal(rsum[:, :], wsum[:, 0, :]).then_inc(G["rsum"], 1)
                    dve.wait_ge(G["attended"], n + 1)
                    dve.wait_ge(G["rsum"], n + 1)
                    nc.vector.tensor_scalar(head_padded[:, 0:KD], head_attended, rsum[:, :], None, ALU.mult)\
                        .then_inc(G["head"], 1)
                    dve.wait_ge(G["mixed"], n + 1)
                    nc.vector.tensor_tensor(X[:, t, :], X[:, t, :], head_mixed, ALU.add).then_inc(G["added"], 1)

                heads_and_tiles(dve, head_operands, tile)
                dve.wait_ge(G["added"], HEADS * TILES + 1)
                for s in range(2):
                    dve.sem_inc(G[f"stored{s}"], 16)
                with dve.Fori(0, TILES // 2) as pair:
                    for s in range(2):
                        t = pair * 2 + s
                        nc.vector.bn_stats(stats3[:, :], X[:, t, :]).then_inc(G["stats"], 1)
                        dve.wait_ge(G["stats"], t + 1)
                        own_instruction(dve, dve_held)
                        nc.vector.bn_aggr(mv3[:, :], stats3[:, :]).then_inc(G["mv"], 1)
                        dve.wait_ge(G["rstd"], t + 1)
                        dve.wait_ge(G[f"stored{s}"], pair * 16 + 16)
                        nc.vector.tensor_scalar(out_tile[:, s, :], X[:, t, :], mv3[:, 0:1], rstd3[:, :],
                                                ALU.subtract, ALU.mult).then_inc(G["normed"], 1)

        @block.tensor
        def _(pe):
            def held_sums(r):
                wait(pe, held_taken, r)
                pe.wait_ge(held_lo_done, r + 1)
                for part in (held_hi[r], held_lo[r]):
                    for q in range(CHUNKS):
                        nc.tensor.matmul(held_rows_out[:, 0, :], ones_r[:, :], part[:, q * BLK:(q + 1) * BLK],
                                         start=part is held_hi[r] and q == 0,
                                         stop=part is held_lo[r] and q == CHUNKS - 1)
                pe.wait_ge(row_counted, r + 1)
                for q in range(CHUNKS):
                    last = nc.tensor.matmul(held_rows_out[:, 1, :], ones_r[:, :], edges[:, q, :],
                                            start=q == 0, stop=q == CHUNKS - 1)
                last.then_inc(held_summed, 1)

            def held_turn(r):
                pe.wait_ge(held_row, r + 1)
                for w in range(2):
                    last = nc.tensor.matmul(held_columns[:, w:w + 1], held_rows[:, w, :], ones[0:1, 0:1],
                                            start=True, stop=True)
                last.then_inc(held_column, 1)

            def transformed(v):
                wait(pe, z_lo, v - 3)
                if v == 1:
                    pe.wait_ge(wvo_ready, DC)
                if v == 2:
                    pe.wait_ge(held_taken, HELD)
                for c in range(DC):
                    last = nc.tensor.matmul(xw_out[v % 4], XT[:, c, v * P:(v + 1) * P], w0_sb[:, c, :],
                                            start=c == 0, stop=c == DC - 1)
                last.then_inc(xw_done, 1)

            pe.wait_ge(ones_ready, 1)
            for r in range(HELD):
                held_sums(r)
                if r == 0:
                    pe.wait_ge(stage_vo_in, 32)
                if r < DC:
                    for k in range(HK // P):
                        last = nc.tensor.matmul(wvo_out[r], stage[:, 0, k * D + r * P:k * D + (r + 1) * P],
                                                stage[:, 1, k * D:(k + 1) * D], start=k == 0, stop=k == HK // P - 1)
                    last.then_inc(wvo_ps, 1)
                if r == 2:
                    pe.wait_ge(xT_in, 32)
                if r >= 2:
                    transformed(r - 2)
                held_turn(r)
            transformed(2)
            transformed(3)
            for v in range(TILES):
                pe.wait_ge(z_lo, v + 1)
                if v + 4 < TILES:
                    transformed(v + 4)
                if v == 0:
                    pe.wait_ge(ident_ready, 1)
                for r in range(HELD):
                    hi, lo = (held[r][:, v * P:(v + 1) * P] for held in (held_hi, held_lo))
                    nc.tensor.matmul(held_acc[r], hi, opA_hi[:, v, :], start=v == 0, stop=False)
                    nc.tensor.matmul(held_acc[r], hi, opA_lo[:, v, :], start=False, stop=False)
                    if v == r:
                        nc.tensor.matmul(held_acc[r], ident_r[:, :], opA_hi[:, v, :], start=False, stop=False)
                        nc.tensor.matmul(held_acc[r], ident_r[:, :], opA_lo[:, v, :], start=False, stop=False)
                    last = nc.tensor.matmul(held_acc[r], lo, opA_hi[:, v, :], start=False, stop=v == TILES - 1)
                    if v == TILES - 1:
                        last.then_inc(L0["acc"], 1)

            def weighted_sum(L, t, s, q, op_hi, op_lo, last_tile_stop):
                pe.wait_ge(L["lo"], t * CHUNKS + q + 1)
                if L is L1:
                    pe.wait_ge(L1["edges"], t * CHUNKS + q + 1)
                for k in range(SUB):
                    j = q * SUB + k
                    hi, lo, edge = (part[:, q, k * P:(k + 1) * P] for part in (part_hi, part_lo, edges))
                    first, end = j == 0, j == TILES - 1
                    nc.tensor.matmul(acc_weighted[s], hi, op_hi[:, j, :], start=first, stop=False)
                    nc.tensor.matmul(acc_weighted[s], hi, op_lo[:, j, :], start=False, stop=False)
                    last = nc.tensor.matmul(acc_weighted[s], lo, op_hi[:, j, :], start=False,
                                            stop=end and last_tile_stop)
                    if L is L1:
                        nc.tensor.matmul(acc_edges[s], edge, op_hi[:, j, :], start=first, stop=False)
                        last = nc.tensor.matmul(acc_edges[s], edge, op_lo[:, j, :], start=False, stop=end)
                last.then_inc(L["chunk_used"], 1)

            def step0(t, s):
                if isinstance(t, int) and t < HELD:
                    return
                pe.wait_ge(L0["branch"], t - HELD + 1 if isinstance(t, int) and t < HELD + 2 else t - 1)
                for q in range(CHUNKS):
                    weighted_sum(L0, t - HELD, s, q, opA_hi, opA_lo, False)
                nc.tensor.matmul(acc_weighted[s], ident_r[:, :], opA_hi[:, t, :], start=False, stop=False)
                nc.tensor.matmul(acc_weighted[s], ident_r[:, :], opA_lo[:, t, :], start=False, stop=True)\
                    .then_inc(L0["acc"], 1)

            over_tiles(pe, step0, peel=HELD + 2)

            pe.wait_ge(w_in, 16 * len(later_weights))

            def queries(t):
                wait(pe, L2["qf"], DC * t)
                if active(t, 4):
                    pe.wait_ge(L2["xT"], t - 3)
                for o in range(DC):
                    for c in range(DC):
                        last = nc.tensor.matmul(q_out[:, o, :], wqT_sb[:, c, o * P:(o + 1) * P],
                                                XT[:, c, tile_cols(t)], start=c == 0, stop=c == DC - 1)
                last.then_inc(L2["q_ps"], 1)

            def scores(u, q):
                for c in range(DC):
                    keys = slice(q * BLK, (q + 1) * BLK)
                    nc.tensor.matmul(wide[:, q, :], q_hi[:, c, :], keyT_hi[:, c, keys], start=c == 0, stop=False)
                    nc.tensor.matmul(wide[:, q, :], q_hi[:, c, :], keyT_lo[:, c, keys], start=False, stop=False)
                    last = nc.tensor.matmul(wide[:, q, :], q_lo[:, c, :], keyT_hi[:, c, keys],
                                            start=False, stop=c == DC - 1)
                last.then_inc(L2["scores"], 1)

            def step1(t, s):
                if isinstance(t, int) and t == TILES + 1:
                    pe.wait_ge(L2["q_lo"], 1)
                    pe.wait_ge(L1["sum"], TILES - 1)
                    pe.wait_ge(L1["key_lo"], DC * (TILES - 4))
                    scores(0, 0)
                    scores(0, 2)
                for q in range(CHUNKS):
                    if q == 1 and isinstance(t, int) and t == TILES:
                        pe.wait_ge(L1["xT_all"], 1)
                        queries(0)
                    if q == 1 and isinstance(t, int) and t == TILES + 1:
                        pe.wait_ge(L1["sum"], TILES)
                        scores(0, 1)
                        pe.wait_ge(L1["xT_all"], 2)
                        queries(1)
                    if active(t, 0):
                        if q == 0:
                            if isinstance(t, int) and t < 2:
                                pe.wait_ge(L0["branch"], TILES - 1 + t)
                            wait(pe, L1["sum"], t - 1)
                        if isinstance(t, int) and t == 0:
                            pe.wait_ge(L0["op_lo"], (q + 1) * SUB)
                        weighted_sum(L1, t, s, q, opB_hi, opB_lo, True)
                    if q == 0 and active(t, 2):
                        v = t - 2
                        pe.wait_ge(L1["xn"], v + 1)
                        wait(pe, L1["xT"], v)
                        for c in range(DC):
                            last = nc.tensor.transpose(xT_out1[:, c, :], xn[:, s, c * P:(c + 1) * P], ident[:, :])
                        last.then_inc(L1["xT_ps"], 1)
                    if q == 2 and active(t, 2):
                        v = t - 2
                        pe.wait_ge(L1["xT"], v + 1)
                        wait(pe, L1["key_lo"], DC * v)
                        wait(pe, L1["value"], v)
                        for o in range(DC):
                            for c in range(DC):
                                last = nc.tensor.matmul(key_out[:, o, :], wkT_sb[:, c, o * P:(o + 1) * P],
                                                        xT_tile[:, s, c, :], start=c == 0, stop=c == DC - 1)
                        last.then_inc(L1["key_ps"], 1)
                        for c in range(DC):
                            last = nc.tensor.matmul(value_out, xT_tile[:, s, c, :], wvT_sb[:, c, :],
                                                    start=c == 0, stop=c == DC - 1)
                        last.then_inc(L1["value_ps"], 1)

            over_tiles(pe, step1, lag=2)
            pe.wait_ge(L1["key_lo"], DC * TILES)
            scores(0, 3)
            pe.wait_ge(L1["value_lo"], TILES)
            pe.wait_ge(L1["xT_all"], TILES)

            def step2(t, s):
                if isinstance(t, int) and t == 2:
                    pe.wait_ge(flag_step, 6)
                    pe.wait_ge(norms_done, 2)
                    nc.tensor.matmul(totals, ones[:, 0:1], sums[:, :], start=True, stop=True)\
                        .then_inc(totals_done, 1)
                if active(t, 2):
                    u = t - 1
                    if active(t, 1):
                        pe.wait_ge(L2["q_lo"], u + 1)
                        for q in range(CHUNKS):
                            pe.wait_ge(L2["masked"], (u - 1) * CHUNKS + q + 1)
                            scores(u, q)
                v = t - 2

                def transpose_weights(q):
                    if q == 0:
                        pe.wait_ge(L2["exp"], v + 1)
                    wait(pe, L2["w_lo"], v * CHUNKS + q - 1)
                    for k in range(SUB):
                        j = q * SUB + k
                        last = nc.tensor.transpose(bank[q % 2][:, k * P:(k + 1) * P],
                                                   raw[:, s, j * P:(j + 1) * P], ident[:, :])
                    last.then_inc(L2["tr_ps"], 1)

                def attend(q):
                    if isinstance(t, int) and t == 2 and q == 0:
                        pe.wait_ge(flag_step, 7)
                    if q == 0:
                        wait(pe, L2["y"], v)
                        wait(pe, L2["y3"], min(v - 1, TILES - 3) if isinstance(v, int) else v - 1)
                    pe.wait_ge(L2["w_lo"], v * CHUNKS + q + 1)
                    for k in range(SUB):
                        j = q * SUB + k
                        hi, lo = (part[:, q, k * P:(k + 1) * P] for part in (part_hi, part_lo))
                        nc.tensor.matmul(attended, hi, opA_hi[:, j, :], start=j == 0, stop=False)
                        nc.tensor.matmul(attended, hi, opA_lo[:, j, :], start=False, stop=False)
                        last = nc.tensor.matmul(attended, lo, opA_hi[:, j, :], start=False, stop=j == TILES - 1)
                    last.then_inc(L2["attended"], 1)

                if active(t, 2):
                    transpose_weights(0)
                    transpose_weights(1)
                def transpose_rows(u):
                    pe.wait_ge(L2["xn"], u + 1)
                    wait(pe, L2["xT"], u)
                    pe.wait_ge(L2["qf"], DC * t if active(t, 0) else DC * TILES)
                    for c in range(DC):
                        last = nc.tensor.transpose(xT_out2[:, c, :], xn[:, 1 - s, c * P:(c + 1) * P], ident[:, :])
                    last.then_inc(L2["xT_ps"], 1)

                def mix(u):
                    pe.wait_ge(L2["xT"], u + 1)
                    wait(pe, L2["y3"], u)
                    if mixed_of(u) is mixed:
                        pe.wait_ge(L2["y"], u + 1)
                    else:
                        pe.wait_ge(L2["masked"], TILES * CHUNKS)
                    for c in range(DC):
                        last = nc.tensor.matmul(mixed_of(u), xT_tile[:, 1 - s, c, :], wvo_sb[:, c, :],
                                                start=c == 0, stop=c == DC - 1)
                    last.then_inc(L2["mixed"], 1)

                last_steps = isinstance(t, int) and t >= TILES
                if active(t, 3) and not last_steps:
                    transpose_rows(t - 3)
                if active(t, 0) and not (isinstance(t, int) and t < 2):
                    queries(t)
                if active(t, 2):
                    attend(0)
                    transpose_weights(2)
                    attend(1)
                    transpose_weights(3)
                    if last_steps:
                        transpose_rows(t - 3)
                    attend(2)
                    if last_steps:
                        mix(t - 3)
                    attend(3)
                elif last_steps:
                    transpose_rows(t - 3)
                    mix(t - 3)
                if active(t, 3) and not last_steps:
                    mix(t - 3)

            over_tiles(pe, step2, lag=3, peel=4)

            with pe.If(needed(pe)):
                def head_operands(h):
                    pe.wait_ge(G["added"], h * TILES + 1)
                    pe.wait_ge(G["weights"], h * 64 + 64)
                    for q in range(CHUNKS):
                        for c in range(DC):
                            last = nc.tensor.matmul(head_key_out[:, q, :], head_wk[:, c, :],
                                                    XT[:, c, q * BLK:(q + 1) * BLK], start=c == 0, stop=c == DC - 1)
                    last.then_inc(G["key_ps"], 1)
                    for j in range(TILES):
                        for c in range(DC):
                            last = nc.tensor.matmul(head_value_out[j // 8][:, j % 8, :], XT[:, c, j * P:(j + 1) * P],
                                                    head_wv[:, c, :], start=c == 0, stop=c == DC - 1)
                    last.then_inc(G["value_ps"], 1)
                    pe.wait_ge(G["key_lo"], h + 1)
                    pe.wait_ge(G["value_lo"], h * 2 + 2)
                    own_instruction(pe, pe_held)

                def tile(n, t):
                    pe.wait_ge(G["added"], n + 1)
                    for c in range(DC):
                        last = nc.tensor.matmul(head_q_out, head_wq[:, c, :], XT[:, c, tile_cols(t)],
                                                start=c == 0, stop=c == DC - 1)
                    last.then_inc(G["q_ps"], 1)
                    pe.wait_ge(G["q_lo"], n + 1)
                    for q in range(CHUNKS):
                        keys = slice(q * BLK, (q + 1) * BLK)
                        nc.tensor.matmul(wide[:, q, :], head_q_hi, head_key_hi[:, keys], start=True, stop=False)
                        nc.tensor.matmul(wide[:, q, :], head_q_hi, head_key_lo[:, keys], start=False, stop=False)
                        last = nc.tensor.matmul(wide[:, q, :], head_q_lo, head_key_hi[:, keys], start=False, stop=True)
                    last.then_inc(G["scores"], 1)
                    pe.wait_ge(G["exp"], n + 1)
                    for q in range(CHUNKS):
                        if q >= 2:
                            pe.wait_ge(G["w_lo"], n * CHUNKS + q - 1)
                        for k in range(SUB):
                            j = q * SUB + k
                            last = nc.tensor.transpose(bank[q % 2][:, k * P:(k + 1) * P],
                                                       scores_sb[:, j * P:(j + 1) * P], ident[:, :])
                        last.then_inc(G["tr_ps"], 1)
                    for q in range(CHUNKS):
                        pe.wait_ge(G["w_lo"], n * CHUNKS + q + 1)
                        for k in range(SUB):
                            j = q * SUB + k
                            hi, lo = (part[:, q, k * P:(k + 1) * P] for part in (part_hi, part_lo))
                            nc.tensor.matmul(head_attended, hi, head_value_hi[:, j, :], start=j == 0, stop=False)
                            nc.tensor.matmul(head_attended, hi, head_value_lo[:, j, :], start=False, stop=False)
                            last = nc.tensor.matmul(head_attended, lo, head_value_hi[:, j, :], start=False,
                                                    stop=j == TILES - 1)
                    last.then_inc(G["attended"], 1)
                    pe.wait_ge(G["head"], n + 1)
                    nc.tensor.transpose(head_T_out, head_padded, ident[:, :]).then_inc(G["head_t_ps"], 1)
                    pe.wait_ge(G["head_t"], n + 1)
                    nc.tensor.matmul(head_mixed, head_T[0:KD, :], head_wo, start=True, stop=True)\
                        .then_inc(G["mixed"], 1)

                heads_and_tiles(pe, head_operands, tile)


def kernel(x, adj, L0_gnn_weight, L2_gnn_Wq, L2_gnn_bq, L2_gnn_Wk, L2_gnn_bk, L2_gnn_Wv, L2_gnn_bv,
           L3_gnn_Wks, L3_gnn_Wqs, L3_gnn_Wvs, L3_gnn_Wo):
    import numpy as np
    import concourse.bacc as bacc
    from concourse.bass_utils import run_bass_kernel_spmd

    x, adj = np.asarray(x), np.asarray(adj)

    def chunked(w):
        w = np.asarray(w)
        return w.reshape(-1, P, w.shape[1]).transpose(1, 0, 2)

    def heads_side_by_side(w):
        return np.asarray(w).transpose(1, 0, 2).reshape(D, HK)

    arrays = dict(
        x=x.reshape(TILES, P, D).transpose(1, 0, 2),
        xT=chunked(x.T),
        adj=adj,
        adjT=adj.reshape(TILES, P, TILES, P).transpose(0, 3, 2, 1).reshape(N, N),
        adj_diag=np.diagonal(adj).reshape(TILES, P).T,
        w0=chunked(L0_gnn_weight),
        wqT=chunked(np.asarray(L2_gnn_Wq).T), bq=np.asarray(L2_gnn_bq).reshape(DC, P).T,
        wkT=chunked(np.asarray(L2_gnn_Wk).T), bk=np.asarray(L2_gnn_bk).reshape(DC, P).T,
        wvT=chunked(np.asarray(L2_gnn_Wv).T), bv=np.broadcast_to(np.asarray(L2_gnn_bv), (P, D)),
        hwk=chunked(heads_side_by_side(L3_gnn_Wks)).reshape(P, -1),
        hwq=chunked(heads_side_by_side(L3_gnn_Wqs)).reshape(P, -1),
        hwv=chunked(heads_side_by_side(L3_gnn_Wvs)).reshape(P, -1),
        hwvT=chunked(heads_side_by_side(L3_gnn_Wvs).T).reshape(P, -1),
        hwo=chunked(np.asarray(L3_gnn_Wo).reshape(HK, D)).reshape(P, -1),
        hwo_rows=np.asarray(L3_gnn_Wo).reshape(HK, D),
        ident_in=np.eye(P, dtype=np.float32),
    )
    nc = bacc.Bacc("TRN2", target_bir_lowering=False, num_devices=1)
    arrays = {name: np.ascontiguousarray(a) for name, a in arrays.items()}
    args = {name: nc.dram_tensor(f"{name}_dram", a.shape, mybir.dt.from_np(a.dtype), kind="ExternalInput").ap()
            for name, a in arrays.items()}
    out = nc.dram_tensor("out_dram", (N, D), F32, kind="ExternalOutput").ap()
    build(nc, out=out, **args)
    r = run_bass_kernel_spmd(nc, [{f"{name}_dram": a for name, a in arrays.items()}], core_ids=[0])
    return r.results[0]["out_dram"]
```
